# Optimizing a Trainium2 kernel written in Bass

```python
import numpy as np
import jax
import jax.numpy as jnp

def _softmax(x, axis=-1):
    return jax.nn.softmax(x, axis=axis)

def _gelu(x):
    return jax.nn.gelu(x, approximate=True)

def _silu(x):
    return jax.nn.silu(x)

def _sigmoid(x):
    return jax.nn.sigmoid(x)

def _layernorm(x, axis=-1, eps=1e-05):
    m = jnp.mean(x, axis=axis, keepdims=True)
    v = jnp.var(x, axis=axis, keepdims=True)
    return (x - m) / jnp.sqrt(v + eps)

def _scatter_add(tgt, idx, src, axis=0):
    return tgt.at[idx].add(src)

def _segment_sum(src, seg, n):
    return jax.ops.segment_sum(src, seg, n)
kernel_name = 'mk_decoder_postln_d2_seqx_r8_3faad3'

def setup_inputs(seed: int=0):
    np.random.seed(seed)
    _w = jnp.asarray

    def _rec_inputs():
        import jax
        import jax.numpy as jnp
        _rk = jax.random.key(seed)
        x = -0.0002928 + 1 * jax.random.normal(jax.random.fold_in(_rk, 1), (8, 256, 128), jnp.float32)
        _lenS = 256 - jax.random.randint(jax.random.fold_in(_rk, 7), (8,), 0, max(1, 256 // 4) + 1, jnp.int32)
        _lenS2 = 256 - jax.random.randint(jax.random.fold_in(_rk, 8), (8,), 0, max(1, 256 // 4) + 1, jnp.int32)
        _ctx_1024P = jax.random.normal(jax.random.fold_in(_rk, 11), (8, 16, 128), jnp.float32)
        _ctx_1024c = jax.random.dirichlet(jax.random.fold_in(_rk, 511), 0.3 * jnp.ones((16,), jnp.float32), (8, 256))
        _ctx_1024t = jnp.einsum('bsk,bkd->bsd', _ctx_1024c, _ctx_1024P)
        _ctx_1024t = _ctx_1024t * jax.lax.rsqrt(jnp.mean(jnp.square(_ctx_1024t)) + 1e-12) * 0.953939
        ctx_1024 = -1.39393e-06 + 0.999914 * (_ctx_1024t + 0.3 * jax.random.normal(jax.random.fold_in(_rk, 611), (8, 256, 128), jnp.float32))
        return (x, ctx_1024)
    x, ctx_1024 = _rec_inputs()

    def _L0_attn_setup():
        import jax, jax.numpy as jnp
        import numpy as np
        HEADS = 64
        DIM_HEAD = 64
        SCALE = DIM_HEAD ** (-0.5)
        EPS = 1e-06
        key = jax.random.key(seed)
        ks = jax.random.split(key, 6)
        b, s, dim = (2, 512, 128)
        inner = HEADS * DIM_HEAD
        std = 0.02
        return {'x': jax.random.normal(ks[0], (b, s, dim), dtype=jnp.float32), 'Wq': jax.random.normal(ks[1], (dim, inner), dtype=jnp.float32) * std, 'Wk': jax.random.normal(ks[2], (dim, inner), dtype=jnp.float32) * std, 'Wv': jax.random.normal(ks[3], (dim, inner), dtype=jnp.float32) * std, 'Wo': jax.random.normal(ks[4], (inner, dim), dtype=jnp.float32) * std, 'bo': jnp.zeros((dim,), dtype=jnp.float32)}
    _L0_attn_all = _L0_attn_setup()
    _L0_attn_in = {k: v for k, v in _L0_attn_all.items() if k in ('Wq', 'Wk', 'Wv', 'Wo', 'bo')}
    del _L0_attn_all

    def _L0_xattn_setup():
        import jax, jax.numpy as jnp
        import numpy as np
        B, T, D, H = (2, 256, 128, 16)
        DH = D // H
        key = jax.random.key(seed)
        ks = jax.random.split(key, 11)
        s = 1.0 / np.sqrt(D)
        return {'q': jax.random.normal(ks[0], (B, T, D), jnp.float32), 'k': jax.random.normal(ks[1], (B, T, D), jnp.float32), 'v': jax.random.normal(ks[2], (B, T, D), jnp.float32), 'wq_w': jax.random.normal(ks[3], (D, D), jnp.float32) * s, 'wq_b': jnp.zeros((D,), jnp.float32), 'wk_w': jax.random.normal(ks[4], (D, D), jnp.float32) * s, 'wk_b': jnp.zeros((D,), jnp.float32), 'wv_w': jax.random.normal(ks[5], (D, D), jnp.float32) * s, 'wv_b': jnp.zeros((D,), jnp.float32), 'wo_w': jax.random.normal(ks[6], (D, D), jnp.float32) * s, 'wo_b': jnp.zeros((D,), jnp.float32)}
    _L0_xattn_all = _L0_xattn_setup()
    _L0_xattn_in = {k: v for k, v in _L0_xattn_all.items() if k in ('wq_w', 'wq_b', 'wk_w', 'wk_b', 'wv_w', 'wv_b', 'wo_w', 'wo_b')}
    del _L0_xattn_all

    def _L0_ffn_setup():
        import jax, jax.numpy as jnp
        import numpy as np
        B, S, D, H, E, K = (4, 128, 128, 256, 8, 2)
        key = jax.random.key(seed)
        ks = jax.random.split(key, 5)
        s = 0.02
        return {'x': jax.random.normal(ks[0], (B, S, D), jnp.float32), 'W1': jax.random.normal(ks[1], (E, H, D), jnp.float32) * s, 'b1': jnp.zeros((E, H), jnp.float32), 'W2': jax.random.normal(ks[2], (E, D, H), jnp.float32) * s, 'b2': jnp.zeros((E, D), jnp.float32), 'Wg': jax.random.normal(ks[3], (E, D), jnp.float32) * s, 'bg': jnp.zeros((E,), jnp.float32)}
    _L0_ffn_all = _L0_ffn_setup()
    _L0_ffn_in = {k: v for k, v in _L0_ffn_all.items() if k in ('W1', 'b1', 'W2', 'b2', 'Wg', 'bg')}
    del _L0_ffn_all

    def _L1_attn_setup():
        import jax, jax.numpy as jnp
        import numpy as np
        import math
        B, L, D_MODEL = (8, 256, 128)
        D_INNER, D_SSM = (256, 128)
        KEY_DIM, VALUE_DIM, H = (96, 192, 4)
        DK, DV = (KEY_DIM // H, VALUE_DIM // H)
        D_CONV = 4
        EPS = 1e-05

        def _dwconv(x, w, b):
            y = jax.lax.conv_general_dilated(x, w, window_strides=(1,), padding=[(1, 2)], dimension_numbers=('NCH', 'OIH', 'NCH'), feature_group_count=x.shape[1])
            return y + b[None, :, None]

        def _l2norm(x):
            return x * jax.lax.rsqrt(jnp.sum(x * x, axis=-1, keepdims=True) + 1e-06)

        def _gated_delta_rule(q, k, v, beta, gk):
            qT = jnp.moveaxis(q, 2, 0)
            kT = jnp.moveaxis(k, 2, 0)
            vT = jnp.moveaxis(v, 2, 0)
            bT = jnp.moveaxis(beta, 2, 0)
            gT = jnp.moveaxis(gk, 2, 0)
            S0 = jnp.zeros((q.shape[0], q.shape[1], q.shape[3], v.shape[3]), q.dtype)

            def step(S, inp):
                qt, kt, vt, bt, gt = inp
                S = S * jnp.exp(gt)[..., None, None]
                u = bt[..., None] * (vt - jnp.einsum('bhk,bhkv->bhv', kt, S))
                S = S + jnp.einsum('bhk,bhv->bhkv', kt, u)
                ot = jnp.einsum('bhk,bhkv->bhv', qt, S)
                return (S, ot)
            _, o = jax.lax.scan(step, S0, (qT, kT, vT, bT, gT))
            return jnp.moveaxis(o, 0, 2)
        key = jax.random.key(seed)
        ks = jax.random.split(key, 20)

        def w(k, shape, fan_in):
            return jax.random.normal(k, shape, jnp.float32) / np.sqrt(fan_in)
        dt = jnp.exp(jax.random.uniform(ks[14], (H,)) * (math.log(0.1) - math.log(0.001)) + math.log(0.001))
        dt = jnp.clip(dt, 0.0001)
        dt_bias = dt + jnp.log(-jnp.expm1(-dt))
        A = jax.random.uniform(ks[13], (H,), minval=0.5, maxval=16.0)
        return {'x': jax.random.normal(ks[0], (B, L, D_MODEL), jnp.float32), 'W_in': w(ks[1], (D_MODEL, D_INNER), D_MODEL), 'conv_x_w': w(ks[2], (D_SSM, 1, D_CONV), D_CONV), 'conv_x_b': jnp.zeros((D_SSM,), jnp.float32), 'conv_z_w': w(ks[3], (D_SSM, 1, D_CONV), D_CONV), 'conv_z_b': jnp.zeros((D_SSM,), jnp.float32), 'W_q': w(ks[4], (D_SSM, KEY_DIM), D_SSM), 'W_k': w(ks[5], (D_SSM, KEY_DIM), D_SSM), 'W_v': w(ks[6], (D_SSM, VALUE_DIM), D_SSM), 'W_g': w(ks[7], (D_SSM, VALUE_DIM), D_SSM), 'W_gk': w(ks[8], (D_SSM, H), D_SSM), 'W_b': w(ks[9], (D_SSM, H), D_SSM), 'b_b': jnp.zeros((H,), jnp.float32), 'A_log': jnp.log(A), 'dt_bias': dt_bias, 'g_norm_w': jnp.ones((DV,), jnp.float32), 'W_so': w(ks[10], (VALUE_DIM, D_SSM), VALUE_DIM), 'W_out': w(ks[11], (D_INNER, D_MODEL), D_INNER)}
    _L1_attn_all = _L1_attn_setup()
    _L1_attn_in = {k: v for k, v in _L1_attn_all.items() if k in ('W_in', 'conv_x_w', 'conv_x_b', 'conv_z_w', 'conv_z_b', 'W_q', 'W_k', 'W_v', 'W_g', 'W_gk', 'W_b', 'b_b', 'A_log', 'dt_bias', 'g_norm_w', 'W_so', 'W_out')}
    del _L1_attn_all

    def _L1_xattn_setup():
        import jax, jax.numpy as jnp
        import numpy as np
        B, S, D = (4, 1024, 128)
        key = jax.random.key(seed)
        ks = jax.random.split(key, 6)
        v = jax.random.normal(ks[0], (B, S, D), dtype=jnp.float32)
        k = jax.random.normal(ks[1], (B, S, D), dtype=jnp.float32)
        q = jax.random.normal(ks[2], (B, S, D), dtype=jnp.float32)
        scale = 1.0 / np.sqrt(D)
        Wq = jax.random.normal(ks[3], (D, D), dtype=jnp.float32) * scale
        Wk = jax.random.normal(ks[4], (D, D), dtype=jnp.float32) * scale
        Wv = jax.random.normal(ks[5], (D, D), dtype=jnp.float32) * scale
        return {'v': v, 'k': k, 'q': q, 'Wq': Wq, 'Wk': Wk, 'Wv': Wv}
    _L1_xattn_all = _L1_xattn_setup()
    _L1_xattn_in = {k: v for k, v in _L1_xattn_all.items() if k in ('Wq', 'Wk', 'Wv')}
    del _L1_xattn_all

    def _L1_ffn_setup():
        import jax, jax.numpy as jnp
        import numpy as np
        D_MODEL = 128
        D_FF = 256
        N_EXPERTS = 8
        TOP_K = 2
        SHARED_MULT = 2
        key = jax.random.key(seed)
        ks = jax.random.split(key, 16)
        s = 0.02
        fs = D_FF * SHARED_MULT
        return {'x': jax.random.normal(ks[0], (2, 256, D_MODEL), dtype=jnp.float32), 'Wg': jax.random.normal(ks[1], (D_MODEL, N_EXPERTS), dtype=jnp.float32) * s, 'W1': jax.random.normal(ks[2], (N_EXPERTS, D_MODEL, D_FF), dtype=jnp.float32) * s, 'b1': jnp.zeros((N_EXPERTS, D_FF), dtype=jnp.float32), 'W3': jax.random.normal(ks[3], (N_EXPERTS, D_MODEL, D_FF), dtype=jnp.float32) * s, 'b3': jnp.zeros((N_EXPERTS, D_FF), dtype=jnp.float32), 'W2': jax.random.normal(ks[4], (N_EXPERTS, D_FF, D_MODEL), dtype=jnp.float32) * s, 'b2': jnp.zeros((N_EXPERTS, D_MODEL), dtype=jnp.float32), 'Ws1': jax.random.normal(ks[5], (D_MODEL, fs), dtype=jnp.float32) * s, 'bs1': jnp.zeros((fs,), dtype=jnp.float32), 'Ws3': jax.random.normal(ks[6], (D_MODEL, fs), dtype=jnp.float32) * s, 'bs3': jnp.zeros((fs,), dtype=jnp.float32), 'Ws2': jax.random.normal(ks[7], (fs, D_MODEL), dtype=jnp.float32) * s, 'bs2': jnp.zeros((D_MODEL,), dtype=jnp.float32)}
    _L1_ffn_all = _L1_ffn_setup()
    _L1_ffn_in = {k: v for k, v in _L1_ffn_all.items() if k in ('Wg', 'W1', 'b1', 'W3', 'b3', 'W2', 'b2', 'Ws1', 'bs1', 'Ws3', 'bs3', 'Ws2', 'bs2')}
    del _L1_ffn_all
    return {'x': x, 'ctx_1024': ctx_1024, 'L0_attn_Wq': _L0_attn_in['Wq'], 'L0_attn_Wk': _L0_attn_in['Wk'], 'L0_attn_Wv': _L0_attn_in['Wv'], 'L0_attn_Wo': _L0_attn_in['Wo'], 'L0_attn_bo': _L0_attn_in['bo'], 'L0_xattn_wq_w': _L0_xattn_in['wq_w'], 'L0_xattn_wq_b': _L0_xattn_in['wq_b'], 'L0_xattn_wk_w': _L0_xattn_in['wk_w'], 'L0_xattn_wk_b': _L0_xattn_in['wk_b'], 'L0_xattn_wv_w': _L0_xattn_in['wv_w'], 'L0_xattn_wv_b': _L0_xattn_in['wv_b'], 'L0_xattn_wo_w': _L0_xattn_in['wo_w'], 'L0_xattn_wo_b': _L0_xattn_in['wo_b'], 'L0_ffn_W1': _L0_ffn_in['W1'], 'L0_ffn_b1': _L0_ffn_in['b1'], 'L0_ffn_W2': _L0_ffn_in['W2'], 'L0_ffn_b2': _L0_ffn_in['b2'], 'L0_ffn_Wg': _L0_ffn_in['Wg'], 'L0_ffn_bg': _L0_ffn_in['bg'], 'L1_attn_W_in': _L1_attn_in['W_in'], 'L1_attn_conv_x_w': _L1_attn_in['conv_x_w'], 'L1_attn_conv_x_b': _L1_attn_in['conv_x_b'], 'L1_attn_conv_z_w': _L1_attn_in['conv_z_w'], 'L1_attn_conv_z_b': _L1_attn_in['conv_z_b'], 'L1_attn_W_q': _L1_attn_in['W_q'], 'L1_attn_W_k': _L1_attn_in['W_k'], 'L1_attn_W_v': _L1_attn_in['W_v'], 'L1_attn_W_g': _L1_attn_in['W_g'], 'L1_attn_W_gk': _L1_attn_in['W_gk'], 'L1_attn_W_b': _L1_attn_in['W_b'], 'L1_attn_b_b': _L1_attn_in['b_b'], 'L1_attn_A_log': _L1_attn_in['A_log'], 'L1_attn_dt_bias': _L1_attn_in['dt_bias'], 'L1_attn_g_norm_w': _L1_attn_in['g_norm_w'], 'L1_attn_W_so': _L1_attn_in['W_so'], 'L1_attn_W_out': _L1_attn_in['W_out'], 'L1_xattn_Wq': _L1_xattn_in['Wq'], 'L1_xattn_Wk': _L1_xattn_in['Wk'], 'L1_xattn_Wv': _L1_xattn_in['Wv'], 'L1_ffn_Wg': _L1_ffn_in['Wg'], 'L1_ffn_W1': _L1_ffn_in['W1'], 'L1_ffn_b1': _L1_ffn_in['b1'], 'L1_ffn_W3': _L1_ffn_in['W3'], 'L1_ffn_b3': _L1_ffn_in['b3'], 'L1_ffn_W2': _L1_ffn_in['W2'], 'L1_ffn_b2': _L1_ffn_in['b2'], 'L1_ffn_Ws1': _L1_ffn_in['Ws1'], 'L1_ffn_bs1': _L1_ffn_in['bs1'], 'L1_ffn_Ws3': _L1_ffn_in['Ws3'], 'L1_ffn_bs3': _L1_ffn_in['bs3'], 'L1_ffn_Ws2': _L1_ffn_in['Ws2'], 'L1_ffn_bs2': _L1_ffn_in['bs2']}

def reference(x, ctx_1024, L0_attn_Wq, L0_attn_Wk, L0_attn_Wv, L0_attn_Wo, L0_attn_bo, L0_xattn_wq_w, L0_xattn_wq_b, L0_xattn_wk_w, L0_xattn_wk_b, L0_xattn_wv_w, L0_xattn_wv_b, L0_xattn_wo_w, L0_xattn_wo_b, L0_ffn_W1, L0_ffn_b1, L0_ffn_W2, L0_ffn_b2, L0_ffn_Wg, L0_ffn_bg, L1_attn_W_in, L1_attn_conv_x_w, L1_attn_conv_x_b, L1_attn_conv_z_w, L1_attn_conv_z_b, L1_attn_W_q, L1_attn_W_k, L1_attn_W_v, L1_attn_W_g, L1_attn_W_gk, L1_attn_W_b, L1_attn_b_b, L1_attn_A_log, L1_attn_dt_bias, L1_attn_g_norm_w, L1_attn_W_so, L1_attn_W_out, L1_xattn_Wq, L1_xattn_Wk, L1_xattn_Wv, L1_ffn_Wg, L1_ffn_W1, L1_ffn_b1, L1_ffn_W3, L1_ffn_b3, L1_ffn_W2, L1_ffn_b2, L1_ffn_Ws1, L1_ffn_bs1, L1_ffn_Ws3, L1_ffn_bs3, L1_ffn_Ws2, L1_ffn_bs2):
    import jax
    import jax.numpy as jnp

    def _L0_attn_ref(x, Wq, Wk, Wv, Wo, bo):
        import jax, jax.numpy as jnp
        import numpy as np
        HEADS = 64
        DIM_HEAD = 64
        SCALE = DIM_HEAD ** (-0.5)
        EPS = 1e-06
        b, s, dim = x.shape
        h, dh = (HEADS, DIM_HEAD)
        q = (x @ Wq).reshape(b, s, h, dh)
        k = (x @ Wk).reshape(b, s, h, dh)
        v = (x @ Wv).reshape(b, s, h, dh)
        q = jax.nn.relu(q) * SCALE
        k = jax.nn.relu(k)
        kv = jnp.einsum('bsid,bsjd->bsdj', k, v)
        out = jnp.einsum('bsid,bsdj->bsij', q, kv)
        q_norm = jnp.einsum('bsid,bsd->bsi', q, k.sum(axis=2))
        out = out / (q_norm[..., None] + EPS)
        out = out.reshape(b, s, h * h)
        return out @ Wo + bo

    def _L0_xattn_ref(q, k, v, wq_w, wq_b, wk_w, wk_b, wv_w, wv_b, wo_w, wo_b):
        import jax, jax.numpy as jnp
        import numpy as np
        B, T, D, H = (2, 256, 128, 16)
        DH = D // H
        b, t, d = q.shape
        wq = (q @ wq_w.T + wq_b).reshape(b, t, H, DH)
        wk = (k @ wk_w.T + wk_b).reshape(b, t, H, DH)
        wv = (v @ wv_w.T + wv_b).reshape(b, t, H, DH)
        scores = jnp.einsum('bthd,bshd->bhts', wq, wk) / jnp.sqrt(jnp.float32(DH))
        probs = jax.nn.softmax(scores, axis=-1)
        attn = jnp.einsum('bhts,bshd->bthd', probs, wv)
        attn = attn.reshape(b, t, d)
        return attn @ wo_w.T + wo_b

    def _L0_ffn_ref(x, W1, b1, W2, b2, Wg, bg):
        import jax, jax.numpy as jnp
        import numpy as np
        B, S, D, H, E, K = (4, 128, 128, 256, 8, 2)
        b, s, d = x.shape
        xt = x.reshape(-1, d)
        gate_logits = xt @ Wg.T + bg
        w, idx = jax.lax.top_k(gate_logits, K)
        w = jax.nn.softmax(w, axis=1)
        h = jax.nn.relu(jnp.einsum('td,ehd->eth', xt, W1) + b1[:, None, :])
        y = jnp.einsum('eth,eoh->eto', h, W2) + b2[:, None, :]
        comb = (jax.nn.one_hot(idx, E, dtype=xt.dtype) * w[..., None]).sum(axis=1)
        out = jnp.einsum('eto,te->to', y, comb)
        return out.reshape(b, s, d)

    def _L1_attn_ref(x, W_in, conv_x_w, conv_x_b, conv_z_w, conv_z_b, W_q, W_k, W_v, W_g, W_gk, W_b, b_b, A_log, dt_bias, g_norm_w, W_so, W_out):
        import jax, jax.numpy as jnp
        import numpy as np
        import math
        B, L, D_MODEL = (8, 256, 128)
        D_INNER, D_SSM = (256, 128)
        KEY_DIM, VALUE_DIM, H = (96, 192, 4)
        DK, DV = (KEY_DIM // H, VALUE_DIM // H)
        D_CONV = 4
        EPS = 1e-05

        def _dwconv(x, w, b):
            y = jax.lax.conv_general_dilated(x, w, window_strides=(1,), padding=[(1, 2)], dimension_numbers=('NCH', 'OIH', 'NCH'), feature_group_count=x.shape[1])
            return y + b[None, :, None]

        def _l2norm(x):
            return x * jax.lax.rsqrt(jnp.sum(x * x, axis=-1, keepdims=True) + 1e-06)

        def _gated_delta_rule(q, k, v, beta, gk):
            qT = jnp.moveaxis(q, 2, 0)
            kT = jnp.moveaxis(k, 2, 0)
            vT = jnp.moveaxis(v, 2, 0)
            bT = jnp.moveaxis(beta, 2, 0)
            gT = jnp.moveaxis(gk, 2, 0)
            S0 = jnp.zeros((q.shape[0], q.shape[1], q.shape[3], v.shape[3]), q.dtype)

            def step(S, inp):
                qt, kt, vt, bt, gt = inp
                S = S * jnp.exp(gt)[..., None, None]
                u = bt[..., None] * (vt - jnp.einsum('bhk,bhkv->bhv', kt, S))
                S = S + jnp.einsum('bhk,bhv->bhkv', kt, u)
                ot = jnp.einsum('bhk,bhkv->bhv', qt, S)
                return (S, ot)
            _, o = jax.lax.scan(step, S0, (qT, kT, vT, bT, gT))
            return jnp.moveaxis(o, 0, 2)
        b, l, _ = x.shape
        xz = jnp.swapaxes(x @ W_in, 1, 2)
        xc, zc = jnp.split(xz, 2, axis=1)
        xs = jax.nn.silu(_dwconv(xc, conv_x_w, conv_x_b))
        zs = jax.nn.silu(_dwconv(zc, conv_z_w, conv_z_b))
        xs = jnp.swapaxes(xs, 1, 2)
        q = (xs @ W_q).reshape(b, l, H, DK).transpose(0, 2, 1, 3)
        k = (xs @ W_k).reshape(b, l, H, DK).transpose(0, 2, 1, 3)
        v = (xs @ W_v).reshape(b, l, H, DV).transpose(0, 2, 1, 3)
        gk = -jnp.exp(A_log) * jax.nn.softplus(xs @ W_gk + dt_bias)
        gk = jnp.swapaxes(gk, 1, 2)
        beta = jnp.swapaxes(jax.nn.sigmoid(xs @ W_b + b_b), 1, 2)
        q = _l2norm(q)
        k = _l2norm(k)
        o = _gated_delta_rule(q, k, v, beta, gk)
        o = o.transpose(0, 2, 1, 3)
        g = (xs @ W_g).reshape(b, l, H, DV)
        o = o * jax.lax.rsqrt(jnp.mean(o * o, axis=-1, keepdims=True) + EPS) * g_norm_w
        o = o * (g * jax.nn.sigmoid(g))
        o = o.reshape(b, l, VALUE_DIM)
        y = o @ W_so
        y = jnp.concatenate([y, jnp.swapaxes(zs, 1, 2)], axis=-1)
        return y @ W_out

    def _L1_xattn_ref(v, k, q, Wq, Wk, Wv):
        import jax, jax.numpy as jnp
        import numpy as np
        B, S, D = (4, 1024, 128)
        q_in = jax.nn.elu(jnp.einsum('bsd,ed->bse', q, Wq)) + 1.0
        k_in = jax.nn.elu(jnp.einsum('bsd,ed->bse', k, Wk)) + 1.0
        v_in = jnp.einsum('bsd,ed->bse', v, Wv)
        kv_in = k_in * v_in
        k_prefix = jnp.cumsum(k_in, axis=1)
        kv_prefix = jnp.cumsum(kv_in, axis=1)
        kv_softmax = (kv_in + kv_prefix) / k_prefix
        return q_in * kv_softmax

    def _L1_ffn_ref(x, Wg, W1, b1, W3, b3, W2, b2, Ws1, bs1, Ws3, bs3, Ws2, bs2):
        import jax, jax.numpy as jnp
        import numpy as np
        D_MODEL = 128
        D_FF = 256
        N_EXPERTS = 8
        TOP_K = 2
        SHARED_MULT = 2
        shape = x.shape
        xf = x.reshape(-1, shape[-1])
        T = xf.shape[0]
        scores = jax.nn.softmax(xf @ Wg, axis=-1)
        ew, eidx = jax.lax.top_k(scores, TOP_K)
        ew = jax.nn.softmax(ew, axis=-1)
        h1 = jnp.einsum('td,edf->etf', xf, W1) + b1[:, None, :]
        h3 = jnp.einsum('td,edf->etf', xf, W3) + b3[:, None, :]
        a = jax.nn.silu(h1 * h3)
        y_all = jnp.einsum('etf,efd->etd', a, W2) + b2[:, None, :]
        comb = jnp.zeros((T, N_EXPERTS), dtype=xf.dtype)
        comb = comb.at[jnp.arange(T)[:, None], eidx].add(ew)
        y = jnp.einsum('etd,te->td', y_all, comb)
        s = jax.nn.silu((xf @ Ws1 + bs1) * (xf @ Ws3 + bs3)) @ Ws2 + bs2
        return (y + s).reshape(shape)
    x = _layernorm(x + _L0_attn_ref(x, L0_attn_Wq, L0_attn_Wk, L0_attn_Wv, L0_attn_Wo, L0_attn_bo), axis=-1)
    x = _layernorm(x + _L0_xattn_ref(x, ctx_1024, ctx_1024, L0_xattn_wq_w, L0_xattn_wq_b, L0_xattn_wk_w, L0_xattn_wk_b, L0_xattn_wv_w, L0_xattn_wv_b, L0_xattn_wo_w, L0_xattn_wo_b), axis=-1)
    x = _layernorm(x + _L0_ffn_ref(x, L0_ffn_W1, L0_ffn_b1, L0_ffn_W2, L0_ffn_b2, L0_ffn_Wg, L0_ffn_bg), axis=-1)
    x = _layernorm(x + _L1_attn_ref(x, L1_attn_W_in, L1_attn_conv_x_w, L1_attn_conv_x_b, L1_attn_conv_z_w, L1_attn_conv_z_b, L1_attn_W_q, L1_attn_W_k, L1_attn_W_v, L1_attn_W_g, L1_attn_W_gk, L1_attn_W_b, L1_attn_b_b, L1_attn_A_log, L1_attn_dt_bias, L1_attn_g_norm_w, L1_attn_W_so, L1_attn_W_out), axis=-1)
    x = _layernorm(x + _L1_xattn_ref(ctx_1024, ctx_1024, x, L1_xattn_Wq, L1_xattn_Wk, L1_xattn_Wv), axis=-1)
    x = _layernorm(x + _L1_ffn_ref(x, L1_ffn_Wg, L1_ffn_W1, L1_ffn_b1, L1_ffn_W3, L1_ffn_b3, L1_ffn_W2, L1_ffn_b2, L1_ffn_Ws1, L1_ffn_bs1, L1_ffn_Ws3, L1_ffn_bs3, L1_ffn_Ws2, L1_ffn_bs2), axis=-1)
    return x

_drawn_inputs = setup_inputs


def setup_inputs(seed=0):
    import zlib

    import numpy as np

    out = dict(_drawn_inputs(seed))
    spreads = {'L0_attn_bo': (0.0, 0.1),
     'L0_xattn_wq_b': (0.0, 0.334),
     'L0_xattn_wk_b': (0.0, 2.0),
     'L0_xattn_wv_b': (0.0, 0.1),
     'L0_xattn_wo_b': (0.0, 0.1),
     'L0_ffn_b1': (0.0, 0.452),
     'L0_ffn_b2': (0.0, 0.1),
     'L0_ffn_bg': (0.0, 0.1),
     'L1_attn_conv_x_b': (0.0, 0.1),
     'L1_attn_conv_z_b': (0.0, 0.1),
     'L1_attn_b_b': (0.0, 0.8),
     'L1_attn_g_norm_w': (1.0, 0.2),
     'L1_ffn_b1': (0.0, 0.8),
     'L1_ffn_b3': (0.0, 0.8),
     'L1_ffn_b2': (0.0, 0.594),
     'L1_ffn_bs1': (0.0, 0.8),
     'L1_ffn_bs3': (0.0, 0.8),
     'L1_ffn_bs2': (0.0, 0.49)}
    factors = {'L0_attn_Wk': 3.887,
     'L1_ffn_W1': 8.0,
     'L1_ffn_W3': 8.0,
     'L1_ffn_W2': 8.0,
     'L1_ffn_Ws1': 4.531,
     'L1_ffn_Ws3': 4.525,
     'L1_ffn_Ws2': 4.065}
    for name, (base, spread) in spreads.items():
        noise = np.random.default_rng([zlib.crc32(name.encode()), seed]).standard_normal(out[name].shape)
        drawn = base * np.exp(spread * noise) if base else spread * noise
        out[name] = jnp.asarray(drawn.astype(out[name].dtype))
    for name, factor in factors.items():
        out[name] = (out[name] * factor).astype(out[name].dtype)
    return out
```

```python
from contextlib import ExitStack

import concourse.bass as bass
from concourse import mybir

F32 = mybir.dt.float32
ALU = mybir.AluOpType
ACT = mybir.ActivationFunctionType
AX = mybir.AxisListType

P = 128
B, S, D = 8, 256, 128
NT = S // P
HA = 64
HALF = P // 2
HX, DX = 16, 8
E = 8
FF = 256
KF = FF // P
NSH = 2
HD, DK, DV = 4, 24, 48
DKP = 32
QK, VD = HD * DK, HD * DV
CONV = 4
LEVELS = 7
GP = 3
LN_EPS, ATT_EPS, L2_EPS = 1e-5, 1e-6, 1e-6
BIG = 3e38

SMALL = [
    ("ident", P), ("upper", P), ("strict", P), ("levels", LEVELS * P), ("headmask", HX), ("blockmask", VD),
    ("fold", P),
    ("ones", P), ("bo", P),
    ("x_wq", P), ("x_wk", P), ("x_wv", P), ("x_wo", P), ("x_bq", 1), ("x_bk", 1), ("x_bv", P), ("x_bo", P),
    ("f_b1", E * KF), ("f_b2", P), ("f_wg", E), ("f_bg", E),
    ("d_win", 2 * P), ("d_cw", 2 * CONV), ("d_cb", 2), ("d_wqkv", 2 * QK + VD + 2 * HD), ("d_wg", VD),
    ("d_bias", 2 * HD), ("d_alog", HD), ("d_gn", DV), ("d_wsoT", VD), ("d_wtop", P), ("d_wbot", P),
    ("p_wq", P), ("p_wk", P), ("p_wv", P),
    ("g_b1", E * KF), ("g_b3", E * KF), ("g_b2", P), ("g_wg", E), ("g_bs1", NSH * KF), ("g_bs3", NSH * KF),
    ("g_bs2", P),
]
AT = {}
_at = 0
for _name, _n in SMALL:
    AT[_name] = (_at, _n)
    _at += _n
NSMALL = _at


def groups():
    out = []
    for first in range(0, HALF // 2, GP):
        for half in range(2):
            out.append((half, first, min(GP, HALF // 2 - first)))
    return out


def build(nc, x, ctx, small, w_qkv, w_o, f_w, g_w, out):
    G = groups()
    NG = len(G)
    with ExitStack() as stack:
        def sb(name, shape):
            return stack.enter_context(nc.sbuf_tensor(name, shape, F32))

        small_sb = sb("small_sb", [P, NSMALL])
        wqkv_sb = sb("wqkv_sb", [P, 3, HA * HA])
        wo_sb = sb("wo_sb", [P, HA // 2, P])
        f_sb = sb("f_sb", [P, 2, E * FF])
        g_sb = sb("g_sb", [P, 3, (E + NSH) * FF])
        wd_sb = sb("wd_sb", [P, 2, P])
        neg_a = sb("neg_a", [P, HD])
        mhalf = sb("mhalf", [P, 8])

        def c(name, rows=P):
            a, n = AT[name]
            return small_sb[0:rows, a:a + n]

        ident = c("ident")
        x_in = sb("x_in", [P, NT, D])
        x_inT = sb("x_inT", [P, S])
        q_sb = sb("q_sb", [P, HALF, HA])
        v_sb = sb("v_sb", [P, HALF // 2, 2 * HA + 1])
        kacc = q_sb[:, 0:8, :].rearrange("p (a b) i -> p a (b i)", a=4)
        ksum = sb("ksum", [P, P])
        rnorm = sb("rnorm", [P, 2, GP])
        handoff = sb("handoff", [P, NT, D])
        f_stat = sb("f_stat", [P, NT, 6])
        f_mv = sb("f_mv", [P, NT, 2])
        ctx_in = sb("ctx_in", [P, NT, D])
        a_ctx = sb("a_ctx", [P, NT, D])
        cxT = sb("cxT", [P, 2, S])
        ctxT, xT = cxT[:, 0, :], cxT[:, 1, :]
        xb = sb("xb", [P, NT, D])
        b_stat = sb("b_stat", [P, NT, 6])
        b_mv = sb("b_mv", [P, NT, 2])
        kqb = sb("kqb", [P, NT, 3, HD, DKP])
        pool = sb("pool", [P, 6528])
        g8 = sb("g8", [P, 8, NT * E])
        rep8 = sb("rep8", [P, NT, 8])
        mx8 = sb("mx8", [P, NT, 8])
        combT = sb("combT", [E, S])

        used = [0]

        def region(*shape, start=None):
            if start is not None:
                used[0] = start
            n = 1
            for k in shape:
                n *= k
            a = pool[:, used[0]:used[0] + n]
            used[0] += n
            assert used[0] <= 6528, used
            if len(shape) == 1:
                return a
            names = "abcd"[:len(shape)]
            kw = {names[i]: shape[i] for i in range(len(shape))}
            return a.rearrange(f"p ({' '.join(names)}) -> p {' '.join(names)}", **kw)

        vm = q_sb[:, :, :].rearrange("p a b -> p (a b)").rearrange("p (t h c) -> p t h c", t=NT, h=HX)
        v_flat = v_sb[:, :, :].rearrange("p a b -> p (a b)")

        def parts_of_v(first, n):
            return v_flat[:, first * S:(first + n) * S]

        qm = parts_of_v(0, 2).rearrange("p (a s) -> p a s", a=2)
        pr = parts_of_v(2, 4).rearrange("p (a t s) -> p a t s", a=2, t=NT)
        pT = parts_of_v(6, 4).rearrange("p (a t s) -> p a t s", a=2, t=NT)
        kT, qT = parts_of_v(10, 1), parts_of_v(11, 1)
        oT = qT
        a_cxT = parts_of_v(12, 2).rearrange("p (a s) -> p a s", a=2)
        nmax = sb("nmax", [P, 2, NT])
        psum_ = sb("psum_", [P, 2, NT])
        prec = sb("prec", [P, 2, NT])
        hs = region(2, KF, S, start=0)
        h1s = region(2, KF, S)
        d_c = region(2, S, start=0)
        d_s = region(2, S)
        d_E = region(HD, P)
        d_MA = region(HD, 2, P)
        d_Bm = region(HD, P)
        d_X = region(HD, P)
        d_XT = region(HD, P)
        d_P = region(HD, P)
        d_kh = region(HD, DKP)
        d_o = region(HD, DV)
        d_sq = region(2 * QK)
        d_t = region(2, HD, DV)
        d_oT = d_X.rearrange("p h s -> p (h s)")[:, 0:2 * P].rearrange("p (a b) -> p a b", a=2)
        d_sm = sb("d_sm", [P, 8, NT, 8])
        side = sb("side", [P, 1536])
        convbuf = side[:, 0:2 * (S + CONV - 1)].rearrange("p (a b) -> p a b", a=2)
        d_kqT = side[:, 0:3 * P].rearrange("p (a b) -> p a b", a=3)
        d_r = side[:, 384:768].rearrange("p (t h v) -> p t h v", t=NT, h=HD)
        d_gs = side[:, 768:1152].rearrange("p (t h v) -> p t h v", t=NT, h=HD)
        d_u = side[:, 1152:1344].rearrange("p (h v) -> p h v", h=HD)
        d_st = side[:, 1344:1536]
        p_k = region(2, S, start=0)
        p_t = region(2, S)
        p_kv = region(S)
        p_kp = region(S)
        p_vp = region(S)

        fb = [stack.enter_context(nc.psum_tensor(f"front{i}", [P, 512], F32)) for i in range(4)]
        bb = [stack.enter_context(nc.psum_tensor(f"back{i}", [P, 512], F32)) for i in range(4)]


        names = """weights_loaded x_loaded ctx_loaded stored wd_psum alog_exp
            front_filled front_act_drained front_dve_drained front_biased front_var front_rstd front_done
            dve_chain handoff_taken 
            x1T_psum a_cxT_ready a_ctx_loaded x1_biased xo_psum cxT_psum cxT_ready vm_zeroed xkq_psum xv_psum xkq_ready xv_ready
            qm_ready scores_ready nmax_ready exp_done sums_inverted probs_ready pT_psum pT_ready pv_done
            oT_ready layer_psum back_var back_rstd normed xT_psum xT_ready
            logits_psum shifted shifted_exp comb_ready combT_psum combT_ready b2_psum b2_taken
            h_psum h_ready y_psum y_added tile_added
            xz_psum conv_zeroed xz_copied conv_done silu_done kqv_psum g_psum squares_done sums_in sums_out
            gates_in gates_exp gates_one gates_ln gates_ready kqb_ready kqT_psum kqT_ready gm_ready decay_psum
            decay_exp decay_ready cum_psum cum_exp kk_psum ma_ready bm_ready p_psum p_copied y2_psum x_updated
            kh_ready r_ready u_psum u_ready o_psum o_ready st_psum st_ready ks_psum gate_silu gate_scaled o_squared
            o_gated oTd_psum oTd_ready
            pkv_psum pq_psum clipped clipped_exp prefix_done
            h3_psum h1_ready prod_ready""".split()
        sem = {n: stack.enter_context(nc.semaphore(n)) for n in names}

        uses = [("xT",)]
        for tile in range(NT):
            uses += [("k", tile, 1, m) for m in range(HA // 8)] + [("ksum", tile)]
            uses += [(kind, tile, w, m) for m in range(HA // 8) for kind, w in (("q", 0), ("v", 2))]
            uses += [("out", tile, half, first, n) for half, first, n in G]
            uses += [("wo", tile)]
        act_drains = [0]
        dve_drains = [0]
        for u in uses:
            act_drains.append(act_drains[-1] + (u[0] == "v"))
            dve_drains.append(dve_drains[-1] + (u[0] != "v"))

        q_pairs = q_sb[:, :, :].rearrange("p (r k) i -> p r (k i)", k=2)

        def front_pe(pe):
            for n, use in enumerate(uses):
                kind, bank = use[0], fb[n % 4]
                if n >= 4:
                    last = n - 4
                    if uses[last][0] == "v":
                        pe.wait_ge(sem["front_act_drained"], act_drains[last + 1])
                    else:
                        pe.wait_ge(sem["front_dve_drained"], dve_drains[last + 1])
                if kind == "xT":
                    pe.wait_ge(sem["x_loaded"], 16)
                    for t in range(NT):
                        mm = nc.tensor.transpose(bank[:, t * P:(t + 1) * P], x_in[:, t, :], ident)
                elif kind in ("q", "k", "v"):
                    _, tile, w, m = use
                    if n == 1:
                        pe.wait_ge(sem["front_dve_drained"], 1)
                    for k in range(4):
                        mm = nc.tensor.matmul(bank[:, k * P:(k + 1) * P], wqkv_sb[:, w, (4 * m + k) * P:(4 * m + k + 1) * P],
                                              x_inT[:, tile * P:(tile + 1) * P], start=True, stop=True)
                elif kind == "ksum":
                    pe.wait_ge(sem["front_dve_drained"], dve_drains[n])
                    for k in range(4):
                        mm = nc.tensor.matmul(bank[:, 0:P], c("fold"), kacc[:, k, :], start=(k == 0), stop=(k == 3))
                elif kind == "out":
                    _, tile, half, first, count = use
                    if first == 0 and half == 0:
                        pe.wait_ge(sem["front_act_drained"], act_drains[n])
                        pe.wait_ge(sem["front_dve_drained"], dve_drains[n])
                    rows = slice(half * HALF, (half + 1) * HALF)
                    w = 2 * HA + 1
                    for k in range(count):
                        mm = nc.tensor.matmul(bank[:, k * w:(k + 1) * w], q_pairs[rows, first + k, :],
                                              v_sb[rows, first + k, :], start=True, stop=True)
                else:
                    pe.wait_ge(sem["front_dve_drained"], dve_drains[n])
                    for j in range(HA // 2):
                        o = q_sb[:, :, :].rearrange("p t (s j) -> p (t s) j", s=2)[:, :, j]
                        mm = nc.tensor.matmul(bank[:, 0:P], o, wo_sb[:, j, :], start=(j == 0), stop=(j == HA // 2 - 1))
                mm.then_inc(sem["front_filled"], 1)
                yield kind
            yield "norm"
            yield from cross_pe(pe)

        def cross_pe(pe):
            pe.wait_ge(sem["a_ctx_loaded"], 16)
            pe.wait_ge(sem["front_done"], 1)
            for t in range(NT):
                nc.tensor.transpose(fb[0][:, halves(t)], a_ctx[:, t, :], ident)
            for t in range(NT):
                mm = nc.tensor.transpose(fb[0][:, halves(NT + t)], handoff[:, t, :], ident)
            mm.then_inc(sem["x1T_psum"], 1)
            yield "xstart"
            pe.wait_ge(sem["a_cxT_ready"], 1)
            nc.tensor.matmul(fb[1][:, 0:S], c("x_wk"), a_cxT[:, 0, :], start=True, stop=True)
            nc.tensor.matmul(fb[1][:, S:2 * S], c("x_wq"), a_cxT[:, 1, :], start=True, stop=True).then_inc(sem["xkq_psum"], 1)
            for t in range(NT):
                mm = nc.tensor.matmul(fb[2][:, halves(t)], a_cxT[:, 0, halves(t)], c("x_wv"), start=True, stop=True)
            mm.then_inc(sem["xv_psum"], 1)
            yield "xproj"
            for k in range(HX + 3):
                if k < HX:
                    pe.wait_ge(sem["xkq_ready"], 1)
                    pe.wait_ge(sem["qm_ready"], k + 1)
                    if k >= 2:
                        pe.wait_ge(sem["exp_done"], k - 1)
                    for t in range(NT):
                        mm = nc.tensor.matmul(fb[k % 2][:, t * S:(t + 1) * S], qm[:, k % 2, halves(t)], kT,
                                              start=True, stop=True)
                    mm.then_inc(sem["scores_ready"], 1)
                if 0 <= k - 2 < HX:
                    j = k - 2
                    pe.wait_ge(sem["probs_ready"], j + 1)
                    pe.wait_ge(sem["xv_ready"], 1)
                    if j:
                        pe.wait_ge(sem["pT_ready"], j)
                    for st in range(NT):
                        for t in range(NT):
                            mm = nc.tensor.transpose(fb[2][:, st * S + t * P:st * S + (t + 1) * P],
                                                     pr[:, j % 2, t, halves(st)], ident)
                    mm.then_inc(sem["pT_psum"], 1)
                if k >= 3:
                    j = k - 3
                    pe.wait_ge(sem["pT_ready"], j + 1)
                    for st in range(NT):
                        mm = nc.tensor.matmul(fb[3][:, 0:S], vm[:, st, j, :], pT[:, j % 2, st, :],
                                              start=(j == 0 and st == 0), stop=(j == HX - 1 and st == NT - 1))
                    mm.then_inc(sem["pv_done"], 1)
                yield "head"
            pe.wait_ge(sem["oT_ready"], 1)
            for t in range(NT):
                mm = nc.tensor.matmul(fb[0][:, halves(t)], oT[:, halves(t)], c("x_wo"), start=True, stop=True)
            mm.then_inc(sem["xo_psum"], 1)
            yield "xout"

        def front_act(act):
            for n, use in enumerate(uses):
                kind, bank = use[0], fb[n % 4]
                if kind == "v":
                    _, tile, w, m = use
                    act.wait_ge(sem["front_filled"], n + 1)
                    for half in range(2):
                        for odd in range(2):
                            src = bank[odd * HALF:(odd + 1) * HALF, :].rearrange("p (m t s) -> p s m t", m=4, s=2)[:, half]
                            dst = v_sb[half * HALF:(half + 1) * HALF, :, 0:2 * HA].rearrange(
                                "p r (k i) -> p r k i", k=2)[:, :, :, 8 * m + odd:8 * m + 8:2].rearrange("p r k m -> p m r k")
                            ins = nc.scalar.activation(dst, src.rearrange("p m (r k) -> p m r k", k=2), ACT.Copy)
                    ins.then_inc(sem["front_act_drained"], 1)
                yield kind
            yield "norm"
            yield from cross_act(act)

        def cross_act(act):
            yield "xstart"
            act.wait_ge(sem["xkq_psum"], 1)
            nc.scalar.activation(kT, fb[1][:, 0:S], ACT.Identity, bias=c("x_bk"))
            nc.scalar.activation(qT, fb[1][:, S:2 * S], ACT.Identity, bias=c("x_bq")).then_inc(sem["xkq_ready"], 1)
            yield "xproj"
            for k in range(HX + 3):
                if k < HX:
                    act.wait_ge(sem["nmax_ready"], k + 1)
                    if k >= 2:
                        act.wait_ge(sem["pT_psum"], k - 1)
                        act.wait_ge(sem["sums_inverted"], k - 1)
                    for t in range(NT):
                        ins = nc.scalar.activation(pr[:, k % 2, t, :], fb[k % 2][:, t * S:(t + 1) * S], ACT.Exp,
                                                   bias=nmax[:, k % 2, t:t + 1], scale=DX ** -0.5,
                                                   accum_out=psum_[:, k % 2, t:t + 1])
                    ins.then_inc(sem["exp_done"], 1)
                yield "head"
            act.wait_ge(sem["pv_done"], HX)
            nc.scalar.activation(oT, fb[3][:, 0:S], ACT.Copy).then_inc(sem["oT_ready"], 1)
            yield "xout"

        def norm_dve(dve, chain, tile_, stat, mv, var, rstd, count):
            for t in range(NT):
                ins = nc.vector.bn_stats(stat[:, t, :], tile_[:, t, :])
            chain(ins)
            for t in range(NT):
                ins = nc.vector.bn_aggr(mv[:, t, :], stat[:, t, :])
            chain(ins)
            nc.vector.tensor_scalar(mv[:, :, 1], mv[:, :, 1], LN_EPS, None, ALU.add).then_inc(sem[var], 1)
            dve.wait_ge(sem[rstd], count)
            for t in range(NT):
                ins = nc.vector.tensor_scalar(tile_[:, t, :], tile_[:, t, :], mv[:, t, 0:1], mv[:, t, 1:2],
                                              ALU.subtract, ALU.mult)
            return ins

        def norm_pool(gps, mv, var, rstd, count):
            gps.wait_ge(sem[var], count)
            nc.gpsimd.tensor_tensor(mv[:, :, 1], mv[:, :, 1], mhalf[:, 0:NT], ALU.pow).then_inc(sem[rstd], 1)

        def front_dve(dve, chain, back_too):
            for n, use in enumerate(uses):
                kind, bank = use[0], fb[n % 4]
                if kind == "v":
                    yield kind
                    continue
                dve.wait_ge(sem["front_filled"], n + 1)
                if kind == "xT":
                    ins = nc.vector.tensor_copy(x_inT[:, :], bank[:, 0:S])
                elif kind == "k":
                    m = use[3]
                    if n == 1:
                        nc.vector.memset(v_sb[:, :, 2 * HA:2 * HA + 1], 1.0)
                    acc = kacc.rearrange("p a t -> p (a t)")
                    if m == 0:
                        ins = nc.vector.tensor_scalar(acc, bank[:, :], 0.0, None, ALU.max)
                    else:
                        dve.wait_ge(sem["front_dve_drained"], dve_drains[n])
                        ins = nc.vector.scalar_tensor_tensor(acc, bank[:, :], 0.0, acc, ALU.max, ALU.add)
                elif kind == "ksum":
                    ins = nc.vector.tensor_scalar(ksum[:, :], bank[:, 0:P], HA ** -0.5, None, ALU.mult)
                elif kind == "q":
                    _, tile, w, m = use
                    if m == 0:
                        dve.wait_ge(sem["front_dve_drained"], dve_drains[n])
                    for half in range(2):
                        for odd in range(2):
                            rows = slice(odd * HALF, (odd + 1) * HALF)
                            src = bank[rows, :].rearrange("p (m t s) -> p s m t", m=4, s=2)[:, half]
                            dst = q_sb[half * HALF:(half + 1) * HALF, :, 8 * m + odd:8 * m + 8:2].rearrange("p t m -> p m t")
                            ks = ksum[rows, half::2].unsqueeze(1).to_broadcast([HALF, 4, HALF])
                            ins = nc.vector.scalar_tensor_tensor(dst, src, 0.0, ks, ALU.max, ALU.mult)
                elif kind == "out":
                    _, tile, half, first, count = use
                    w = 2 * HA + 1
                    src = bank[:, 0:count * w].rearrange("p (r i) -> p r i", i=w)
                    rn = rnorm[:, n % 2, 0:count]
                    chain(nc.vector.tensor_scalar(rn, src[:, :, 2 * HA], ATT_EPS, None, ALU.add))
                    chain(nc.vector.reciprocal(rn, rn))
                    if half == 0:
                        dve.wait_ge(sem["front_filled"], n + 2)
                    for tok in range(2):
                        for jh in range(2):
                            lo = tok * HALF
                            dst = q_sb[jh * HALF:(jh + 1) * HALF, 2 * first + tok:2 * (first + count) + tok - 1:2,
                                       half * 32:half * 32 + 32]
                            ins = nc.vector.tensor_tensor(
                                dst, src[lo:lo + HALF, :, tok * HA + jh * 32:tok * HA + jh * 32 + 32],
                                rn[lo:lo + HALF].unsqueeze(2).to_broadcast([HALF, count, 32]), ALU.mult)
                else:
                    if use[1] == 0:
                        dve.wait_ge(sem["front_biased"], 1)
                        if back_too:
                            dve.wait_ge(sem["handoff_taken"], 1)
                    ins = nc.vector.tensor_tensor(handoff[:, use[1], :], bank[:, 0:P], x_in[:, use[1], :], ALU.add)
                ins.then_inc(sem["front_dve_drained"], 1)
                yield kind
            dve.wait_ge(sem["front_dve_drained"], dve_drains[-1])
            norm_dve(dve, chain, handoff, f_stat, f_mv, "front_var", "front_rstd", 1).then_inc(sem["front_done"], 1)
            yield "norm"
            yield from cross_dve(dve, chain)

        def cross_dve(dve, chain):
            dve.wait_ge(sem["x1T_psum"], 1)
            nc.vector.tensor_copy(a_cxT.rearrange("p a s -> p (a s)"), fb[0][:, :]).then_inc(sem["a_cxT_ready"], 1)
            nc.vector.tensor_tensor(handoff[:, :, :], handoff[:, :, :], c("x_bo").unsqueeze(1).to_broadcast([P, NT, D]),
                                    ALU.add).then_inc(sem["x1_biased"], 1)
            yield "xstart"
            dve.wait_ge(sem["xv_psum"], 1)
            dve.wait_ge(sem["vm_zeroed"], 1)
            step = P + DX
            for t in range(NT):
                flat = vm[:, t].rearrange("p h c -> p (h c)")
                n = HX - 1
                nc.vector.tensor_tensor(flat[:, 0:n * step].rearrange("p (h c) -> p h c", c=step)[:, :, 0:DX],
                                        fb[2][:, t * P:t * P + n * DX].rearrange("p (h d) -> p h d", d=DX),
                                        c("x_bv")[:, 0:n * DX].rearrange("p (h d) -> p h d", d=DX), ALU.add)
                ins = nc.vector.tensor_tensor(flat[:, n * step:n * step + DX], fb[2][:, t * P + n * DX:(t + 1) * P],
                                              c("x_bv")[:, n * DX:P], ALU.add)
            ins.then_inc(sem["xv_ready"], 1)
            yield "xproj"
            for k in range(HX + 3):
                if k < HX:
                    dve.wait_ge(sem["scores_ready"], k + 1)
                    chain(nc.vector.tensor_reduce(nmax[:, k % 2, :], fb[k % 2][:, :].rearrange("p (t s) -> p t s", t=NT),
                                                  AX.X, ALU.max, negate=True))
                    nc.vector.tensor_scalar(nmax[:, k % 2, :], nmax[:, k % 2, :], DX ** -0.5, None,
                                            ALU.mult).then_inc(sem["nmax_ready"], 1)
                if 1 <= k <= HX:
                    j = k - 1
                    dve.wait_ge(sem["exp_done"], j + 1)
                    if j >= 2:
                        dve.wait_ge(sem["probs_ready"], j - 1)
                    nc.vector.reciprocal(prec[:, j % 2, :], psum_[:, j % 2, :]).then_inc(sem["sums_inverted"], 1)
                if 0 <= k - 2 < HX:
                    j = k - 2
                    dve.wait_ge(sem["pT_psum"], j + 1)
                    if j >= 2:
                        dve.wait_ge(sem["pv_done"], j - 1)
                    nc.vector.tensor_copy(pT[:, j % 2].rearrange("p a s -> p (a s)"), fb[2][:, :]).then_inc(sem["pT_ready"], 1)
                yield "head"
            dve.wait_ge(sem["xo_psum"], 1)
            dve.wait_ge(sem["x1_biased"], 1)
            x1 = handoff[:, :, :].rearrange("p t d -> p (t d)")
            chain(nc.vector.tensor_tensor(x1, fb[0][:, 0:S], x1, ALU.add))
            norm_dve(dve, chain, handoff, f_stat, f_mv, "front_var", "front_rstd", 2)
            yield "xout"

        def front_pool(gps):
            for n, use in enumerate(uses):
                if n == 0:
                    gps.wait_ge(sem["front_filled"], 1)
                    nc.gpsimd.tensor_tensor(x_in[:, :, :], x_in[:, :, :],
                                            c("bo").unsqueeze(1).to_broadcast([P, NT, D]), ALU.add).then_inc(sem["front_biased"], 1)
                yield use[0]
            norm_pool(gps, f_mv, "front_var", "front_rstd", 1)
            yield "norm"
            yield from cross_pool(gps)

        def cross_pool(gps):
            gps.wait_ge(sem["front_filled"], len(uses))
            nc.gpsimd.memset(vm.rearrange("p t h c -> p (t h c)"), 0.0).then_inc(sem["vm_zeroed"], 1)
            yield "xstart"

            def head_queries(k):
                if k >= 2:
                    gps.wait_ge(sem["scores_ready"], k - 1)
                nc.gpsimd.tensor_scalar(qm[:, k % 2, :], qT, c("headmask")[:, k:k + 1], None, ALU.mult).then_inc(sem["qm_ready"], 1)

            gps.wait_ge(sem["xkq_ready"], 1)
            head_queries(0)
            yield "xproj"
            for k in range(HX + 3):
                if k + 1 < HX:
                    head_queries(k + 1)
                if 1 <= k <= HX:
                    j = k - 1
                    gps.wait_ge(sem["sums_inverted"], j + 1)
                    for t in range(NT):
                        ins = nc.gpsimd.tensor_scalar(pr[:, j % 2, t, :], pr[:, j % 2, t, :], prec[:, j % 2, t:t + 1], None, ALU.mult)
                    ins.then_inc(sem["probs_ready"], 1)
                yield "head"
            norm_pool(gps, f_mv, "front_var", "front_rstd", 2)
            yield "xout"

        def halves(k):
            return slice(k * P, (k + 1) * P)

        def turn_pe(pe, count):
            pe.wait_ge(sem["normed"], count)
            for t in range(NT):
                mm = nc.tensor.transpose(bb[1][:, halves(t)], xb[:, t, :], ident)
            mm.then_inc(sem["xT_psum"], 1)

        def gate_pe(pe, count, wg, b2):
            pe.wait_ge(sem["cxT_ready" if count == 1 else "xT_ready"], 1 if count == 1 else 3)
            for t in range(NT):
                mm = nc.tensor.matmul(bb[2][:, t * E:(t + 1) * E], xT[:, halves(t)], wg, start=True, stop=True)
            mm.then_inc(sem["logits_psum"], 1)
            yield "gate"
            pe.wait_ge(sem["comb_ready"], count)
            for t in range(NT):
                mm = nc.tensor.transpose(bb[3][0:E, halves(t)], g8[:, 4, t * E:(t + 1) * E], ident)
            mm.then_inc(sem["combT_psum"], 1)
            yield "combT"
            pe.wait_ge(sem["combT_ready"], count)
            for t in range(NT):
                mm = nc.tensor.matmul(bb[2][:, halves(t)], combT[:, halves(t)], b2, start=True, stop=True)
            mm.then_inc(sem["b2_psum"], 1)
            yield "b2"

        def back_pe(pe):
            pe.wait_ge(sem["ctx_loaded"], 16)
            for t in range(NT):
                nc.tensor.transpose(bb[0][:, halves(t)], ctx_in[:, t, :], ident)
            for t in range(NT):
                mm = nc.tensor.transpose(bb[0][:, halves(NT + t)], handoff[:, t, :], ident)
            mm.then_inc(sem["cxT_psum"], 1)
            yield "start"
            yield from gate_pe(pe, 1, c("f_wg"), c("f_b2", E))
            for e in range(E + 1):
                if e < E:
                    if e >= 2:
                        pe.wait_ge(sem["h_ready"], e - 1)
                    for kf in range(KF):
                        a = e * FF + kf * P
                        mm = nc.tensor.matmul(bb[e % 2][:, kf * S:(kf + 1) * S], f_sb[:, 0, a:a + P], xT,
                                              start=True, stop=True)
                    mm.then_inc(sem["h_psum"], 1)
                if e:
                    j = e - 1
                    pe.wait_ge(sem["h_ready"], j + 1)
                    pe.wait_ge(sem["b2_taken"], 1)
                    if j >= 2:
                        pe.wait_ge(sem["y_added"], j - 1)
                    for t in range(NT):
                        for kf in range(KF):
                            a = (j * KF + kf) * P
                            mm = nc.tensor.matmul(bb[2 + j % 2][:, halves(t)], hs[:, j % 2, kf, halves(t)],
                                                  f_sb[:, 1, a:a + P], start=(kf == 0), stop=(kf == KF - 1))
                    mm.then_inc(sem["y_psum"], 1)
                yield "expert"
            yield "norm"
            turn_pe(pe, 1)
            yield "turn"
            pe.wait_ge(sem["xT_ready"], 1)
            for a in range(2):
                mm = nc.tensor.matmul(bb[0][:, a * S:(a + 1) * S], c("d_win")[:, halves(a)], xT, start=True, stop=True)
            mm.then_inc(sem["xz_psum"], 1)
            yield "dproj"
            pe.wait_ge(sem["silu_done"], 1)
            for t in range(NT):
                w = 2 * QK + VD + 2 * HD
                nc.tensor.matmul(bb[1 + t][:, 0:w], d_s[:, 0, halves(t)], c("d_wqkv"), start=True,
                                 stop=True).then_inc(sem["kqv_psum"], 1)
            for t in range(NT):
                mm = nc.tensor.matmul(bb[3][:, t * VD:(t + 1) * VD], d_s[:, 0, halves(t)], c("d_wg"), start=True, stop=True)
            mm.then_inc(sem["g_psum"], 1)
            yield "dtok"
            yield "dgates"
            for t in range(NT):
                pe.wait_ge(sem["gm_ready"], t + 1)
                nc.tensor.matmul(bb[0][:, :], c("strict"), d_Bm.rearrange("p h t -> p (h t)"), start=True,
                                 stop=True).then_inc(sem["decay_psum"], 1)
                pe.wait_ge(sem["kqb_ready"], NT)
                for a in range(3):
                    mm = nc.tensor.transpose(bb[1][:, halves(a)], kqb[:, t, a].rearrange("p h d -> p (h d)"), ident)
                mm.then_inc(sem["kqT_psum"], 1)
                if t:
                    nc.tensor.matmul(bb[2][:, 0:HD], c("upper"), d_sm[:, 5, t, 0:HD], start=True,
                                     stop=True).then_inc(sem["cum_psum"], 1)
                yield "decay"
                pe.wait_ge(sem["kqT_ready"], t + 1)
                pe.wait_ge(sem["decay_exp"], t + 1)
                pe.wait_ge(sem["gate_silu"], 1)
                if t:
                    pe.wait_ge(sem["cum_exp"], 1)
                    pe.wait_ge(sem["tile_added"], t)
                for h in range(HD):
                    rows = slice(h * DKP, (h + 1) * DKP)
                    nc.tensor.matmul(bb[h][:, 0:2 * P], d_kqT[rows, 0, :], d_kqT[rows, 1:3, :], start=True,
                                     stop=True).then_inc(sem["kk_psum"], 1)
                yield "kk"
                pe.wait_ge(sem["ma_ready"], HD * (t + 1))
                if t:
                    pe.wait_ge(sem["st_ready"], 1)
                    nc.tensor.matmul(bb[3][:, 0:VD], d_kqT[:, 2, :], d_st, start=True, stop=True)
                    nc.tensor.matmul(bb[3][:, VD:2 * VD], d_kqT[:, 1, :], d_st, start=True,
                                     stop=True).then_inc(sem["ks_psum"], 1)
                for l in range(LEVELS):
                    pe.wait_ge(sem["bm_ready"], LEVELS * t + l + 1)
                    if l:
                        pe.wait_ge(sem["x_updated"], LEVELS * t + l)
                    for h in range(HD):
                        mm = nc.tensor.matmul(bb[0][:, halves(h)], d_Bm[:, h, :], d_X[:, h, :] if l else ident,
                                              start=True, stop=True)
                    mm.then_inc(sem["p_psum"], 1)
                    yield "level"
                    if l:
                        pe.wait_ge(sem["p_copied"], (LEVELS - 1) * t + l)
                        if l < LEVELS - 1:
                            for h in range(HD):
                                mm = nc.tensor.matmul(bb[1][:, halves(h)], d_XT[:, h, :], d_P[:, h, :], start=True, stop=True)
                            mm.then_inc(sem["y2_psum"], 1)
                        for h in range(HD):
                            mm = nc.tensor.matmul(bb[2][:, halves(h)], d_P[:, h, :], d_XT[:, h, :], start=True, stop=True)
                        mm.then_inc(sem["y2_psum"], 1)
                    yield "level2"
                pe.wait_ge(sem["x_updated"], LEVELS * (t + 1))
                if t:
                    pe.wait_ge(sem["r_ready"], t)
                for h in range(HD):
                    mm = nc.tensor.matmul(bb[0][:, h * DV:(h + 1) * DV], d_XT[:, h, :], d_r[:, t, h, :], start=True, stop=True)
                mm.then_inc(sem["u_psum"], 1)
                yield "u"
                pe.wait_ge(sem["u_ready"], t + 1)
                for h in range(HD):
                    mm = nc.tensor.matmul(bb[1][:, h * DV:(h + 1) * DV], d_MA[:, h, 0, :], d_u[:, h, :], start=True, stop=True)
                mm.then_inc(sem["o_psum"], 1)
                if t == 0:
                    pe.wait_ge(sem["kh_ready"], 1)
                    nc.tensor.matmul(bb[3][:, 0:VD], d_kh.rearrange("p h d -> p (h d)"), d_u.rearrange("p h v -> p (h v)"),
                                     start=True, stop=True).then_inc(sem["st_psum"], 1)
                yield "o"
                pe.wait_ge(sem["o_gated"], t + 1)
                of = d_o.rearrange("p h v -> p (h v)")
                nc.tensor.transpose(bb[2][:, 0:P], of[:, 0:P], ident)
                nc.tensor.transpose(bb[2][0:VD - P, P:2 * P], of[:, P:VD], ident).then_inc(sem["oTd_psum"], 1)
                yield "oT"
                pe.wait_ge(sem["oTd_ready"], t + 1)
                if t == 0:
                    pe.wait_ge(sem["st_ready"], 1)
                pe.wait_ge(sem["silu_done"], 2)
                nc.tensor.matmul(bb[3][:, 0:P], d_oT[:, 0, :], wd_sb[:, 0, :], start=True, stop=False)
                nc.tensor.matmul(bb[3][:, 0:P], d_s[:, 1, halves(t)], c("d_wbot"), start=False, stop=False)
                nc.tensor.matmul(bb[3][:, 0:P], d_oT[0:VD - P, 1, :], wd_sb[0:VD - P, 1, :], start=False,
                                 stop=True).then_inc(sem["layer_psum"], 1)
                yield "dout"
            yield "norm"
            turn_pe(pe, 2)
            nc.tensor.matmul(bb[0][:, 0:S], c("p_wk"), ctxT, start=True, stop=True)
            nc.tensor.matmul(bb[0][:, S:2 * S], c("p_wv"), ctxT, start=True, stop=True).then_inc(sem["pkv_psum"], 1)
            yield "turn"
            pe.wait_ge(sem["xT_ready"], 2)
            nc.tensor.matmul(bb[2][:, 0:S], c("p_wq"), xT, start=True, stop=True).then_inc(sem["pq_psum"], 1)
            yield "prefix"
            pe.wait_ge(sem["prefix_done"], 1)
            for t in range(NT):
                mm = nc.tensor.transpose(bb[3][:, halves(t)], p_vp[:, halves(t)], ident)
            mm.then_inc(sem["layer_psum"], 1)
            yield "pout"
            turn_pe(pe, 3)
            yield "turn"
            yield from gate_pe(pe, 2, c("g_wg"), c("g_b2", E))
            for e in range(E + NSH + 2):
                if e < E + NSH:
                    if e:
                        pe.wait_ge(sem["h1_ready"], e)
                    for kf in range(KF):
                        a = e * FF + kf * P
                        mm = nc.tensor.matmul(bb[0][:, kf * S:(kf + 1) * S], g_sb[:, 0, a:a + P], xT, start=True, stop=True)
                    mm.then_inc(sem["h_psum"], 1)
                    if e:
                        pe.wait_ge(sem["prod_ready"], e)
                    for kf in range(KF):
                        a = e * FF + kf * P
                        mm = nc.tensor.matmul(bb[1][:, kf * S:(kf + 1) * S], g_sb[:, 1, a:a + P], xT, start=True, stop=True)
                    mm.then_inc(sem["h3_psum"], 1)
                if e >= 2:
                    j = e - 2
                    pe.wait_ge(sem["h_ready"], E + j + 1)
                    pe.wait_ge(sem["b2_taken"], 2)
                    if j >= 2:
                        pe.wait_ge(sem["y_added"], E + j - 1)
                    for t in range(NT):
                        for kf in range(KF):
                            a = (j * KF + kf) * P
                            mm = nc.tensor.matmul(bb[2 + j % 2][:, halves(t)], hs[:, j % 2, kf, halves(t)],
                                                  g_sb[:, 2, a:a + P], start=(kf == 0), stop=(kf == KF - 1))
                    mm.then_inc(sem["y_psum"], 1)
                yield "gexpert"
            yield "norm"

        def turn_act(act, count):
            act.wait_ge(sem["xT_psum"], count)
            nc.scalar.activation(xT, bb[1][:, 0:S], ACT.Copy).then_inc(sem["xT_ready"], 1)

        def gate_act(act, count, shifts):
            for n in shifts:
                act.wait_ge(sem["shifted"], n)
                nc.scalar.activation(g8[:, 3, :], g8[:, 3, :], ACT.Exp).then_inc(sem["shifted_exp"], 1)
            yield "gate"
            act.wait_ge(sem["combT_psum"], count)
            nc.scalar.activation(combT[:, :], bb[3][0:E, 0:S], ACT.Copy).then_inc(sem["combT_ready"], 1)
            yield "combT"
            yield "b2"

        def back_act(act):
            yield "start"
            yield from gate_act(act, 1, (1,))
            for e in range(E + 1):
                if e < E:
                    act.wait_ge(sem["h_psum"], e + 1)
                    if e >= 2:
                        act.wait_ge(sem["y_psum"], e - 1)
                    for kf in range(KF):
                        n = e * KF + kf
                        ins = nc.scalar.activation(hs[:, e % 2, kf, :], bb[e % 2][:, kf * S:(kf + 1) * S], ACT.Relu,
                                                   bias=c("f_b1")[:, n:n + 1])
                    ins.then_inc(sem["h_ready"], 1)
                yield "expert"
            yield "norm"
            turn_act(act, 1)
            yield "turn"
            act.wait_ge(sem["xz_psum"], 1)
            nc.scalar.activation(convbuf[:, :, 1:S + 1], bb[0][:, :].rearrange("p (a t) -> p a t", a=2),
                                 ACT.Copy).then_inc(sem["xz_copied"], 1)
            for a in range(2):
                act.wait_ge(sem["conv_done"], a + 1)
                nc.scalar.activation(d_s[:, a, :], d_c[:, a, :], ACT.Silu, bias=c("d_cb")[:, a:a + 1]).then_inc(sem["silu_done"], 1)
            yield "dproj"
            act.wait_ge(sem["g_psum"], 1)
            nc.scalar.activation(d_gs.rearrange("p t h v -> p (t h v)"), bb[3][:, 0:NT * VD], ACT.Silu).then_inc(sem["gate_silu"], 1)
            for t in range(NT):
                act.wait_ge(sem["kqv_psum"], t + 1)
                if t:
                    act.wait_ge(sem["sums_in"], t)
                nc.scalar.activation(d_sq, bb[1 + t][:, 0:2 * QK], ACT.Square).then_inc(sem["squares_done"], 1)
            yield "dtok"
            act.wait_ge(sem["gates_in"], 1)
            nc.scalar.activation(d_sm[:, 3], d_sm[:, 3], ACT.Exp).then_inc(sem["gates_exp"], 1)
            act.wait_ge(sem["gates_one"], 1)
            nc.scalar.activation(d_sm[:, 4, :, 0:HD], d_sm[:, 3, :, 0:HD], ACT.Ln).then_inc(sem["gates_ln"], 1)
            yield "dgates"
            for t in range(NT):
                act.wait_ge(sem["decay_psum"], t + 1)
                nc.scalar.activation(d_E.rearrange("p h t -> p (h t)"), bb[0][:, :], ACT.Exp).then_inc(sem["decay_exp"], 1)
                act.wait_ge(sem["kqT_psum"], t + 1)
                nc.scalar.activation(d_kqT, bb[1][:, 0:3 * P].rearrange("p (a b) -> p a b", a=3), ACT.Copy).then_inc(sem["kqT_ready"], 1)
                if t:
                    act.wait_ge(sem["cum_psum"], 1)
                    nc.scalar.activation(d_sm[:, 6, 0, 0:HD], bb[2][:, 0:HD], ACT.Exp).then_inc(sem["cum_exp"], 1)
                yield "decay"
                yield "kk"
                for l in range(LEVELS):
                    if l:
                        act.wait_ge(sem["p_psum"], LEVELS * t + l + 1)
                        nc.scalar.activation(d_P.rearrange("p h t -> p (h t)"), bb[0][:, :], ACT.Copy).then_inc(sem["p_copied"], 1)
                    yield "level"
                    yield "level2"
                yield "u"
                act.wait_ge(sem["o_ready"], t + 1)
                nc.scalar.activation(d_sq[:, 0:VD], d_o.rearrange("p h v -> p (h v)"), ACT.Square).then_inc(sem["o_squared"], 1)
                yield "o"
                act.wait_ge(sem["oTd_psum"], t + 1)
                nc.scalar.activation(d_oT[:, 0, :], bb[2][:, 0:P], ACT.Copy)
                nc.scalar.activation(d_oT[0:VD - P, 1, :], bb[2][0:VD - P, P:2 * P], ACT.Copy).then_inc(sem["oTd_ready"], 1)
                yield "oT"
                yield "dout"
            yield "norm"
            turn_act(act, 2)
            yield "turn"
            for a in range(2):
                act.wait_ge(sem["clipped"], a + 1)
                nc.scalar.activation(p_t[:, a, :], p_t[:, a, :], ACT.Exp).then_inc(sem["clipped_exp"], 1)
            yield "prefix"
            yield "pout"
            turn_act(act, 3)
            yield "turn"
            yield from gate_act(act, 2, (2, 3))
            for e in range(E + NSH + 2):
                if e < E + NSH:
                    act.wait_ge(sem["h_psum"], E + e + 1)
                    if e >= 2:
                        act.wait_ge(sem["h_ready"], E + e - 1)
                    b1 = c("g_b1") if e < E else c("g_bs1")
                    for kf in range(KF):
                        n = (e if e < E else e - E) * KF + kf
                        ins = nc.scalar.activation(h1s[:, e % 2, kf, :], bb[0][:, kf * S:(kf + 1) * S], ACT.Identity,
                                                   bias=b1[:, n:n + 1])
                    ins.then_inc(sem["h1_ready"], 1)
                if 1 <= e <= E + NSH:
                    j = e - 1
                    act.wait_ge(sem["prod_ready"], j + 1)
                    if j >= 2:
                        act.wait_ge(sem["y_psum"], E + j - 1)
                    nc.scalar.activation(hs[:, j % 2], h1s[:, j % 2], ACT.Silu).then_inc(sem["h_ready"], 1)
                yield "gexpert"
            yield "norm"

        def top2_dve(dve, chain, src, count, shift):
            for t in range(NT):
                ins = nc.vector.max(mx8[:, t, :], src[:, t * E:(t + 1) * E])
            chain(ins)
            chain(nc.vector.tensor_copy(rep8[:, :, 0:2], mx8[:, :, 0:2]))
            for t in range(NT):
                one = slice(t * E, (t + 1) * E)
                nc.vector.match_replace(g8[:, 1, one], rep8[:, t, :], src[:, one], -BIG)
                ins = nc.vector.tensor_scalar(g8[:, 3, one], src[:, one], mx8[:, t, 0:1], None, ALU.subtract)
            ins.then_inc(sem["shifted"], 1)
            dve.wait_ge(sem["shifted"], shift)
            chain(nc.vector.tensor_tensor(g8[:, 2, :], g8[:, 1, :], src, ALU.not_equal))
            dve.wait_ge(sem["shifted_exp"], shift)
            chain(nc.vector.tensor_tensor(g8[:, 4, :], g8[:, 3, :], g8[:, 2, :], ALU.mult))
            share_dve(chain, g8[:, 4, :], g8[:, 4, :]).then_inc(sem["comb_ready"], 1)

        def share_dve(chain, dst, src):
            s8 = src.rearrange("p (t e) -> p t e", t=NT)
            tot = g8[:, 6, 0:NT]
            chain(nc.vector.tensor_reduce(tot, s8, AX.X, ALU.add))
            chain(nc.vector.reciprocal(tot, tot))
            return nc.vector.tensor_tensor(dst.rearrange("p (t e) -> p t e", t=NT), s8,
                                           tot.unsqueeze(2).to_broadcast([P, NT, E]), ALU.mult)

        def back_norm_dve(dve, chain, count):
            norm_dve(dve, chain, xb, b_stat, b_mv, "back_var", "back_rstd", count).then_inc(sem["normed"], 1)

        def back_dve(dve, chain):
            xf = xb[:, :, :].rearrange("p t d -> p (t d)")
            dve.wait_ge(sem["cxT_psum"], 1)
            nc.vector.tensor_copy(cxT[:, :, :].rearrange("p a s -> p (a s)"), bb[0][:, :]).then_inc(sem["cxT_ready"], 1)
            nc.vector.tensor_copy(xb[:, :, :], handoff[:, :, :]).then_inc(sem["handoff_taken"], 1)
            dve.wait_ge(sem["handoff_taken"], 1)
            yield "start"
            dve.wait_ge(sem["logits_psum"], 1)
            chain(nc.vector.tensor_tensor(g8[:, 0, :].rearrange("p (t e) -> p t e", t=NT),
                                          bb[2][:, 0:NT * E].rearrange("p (t e) -> p t e", t=NT),
                                          c("f_bg").unsqueeze(1).to_broadcast([P, NT, E]), ALU.add))
            top2_dve(dve, chain, g8[:, 0, :], 1, 1)
            yield "gate"
            yield "combT"
            dve.wait_ge(sem["b2_psum"], 1)
            nc.vector.tensor_tensor(xf, bb[2][:, 0:S], xf, ALU.add).then_inc(sem["b2_taken"], 1)
            dve.wait_ge(sem["b2_taken"], 1)
            yield "b2"
            for e in range(E + 1):
                if e:
                    add_expert(dve, e - 1, e - 1)
                yield "expert"
            dve.wait_ge(sem["y_added"], E)
            back_norm_dve(dve, chain, 1)
            yield "norm"
            yield "turn"
            dve.wait_ge(sem["xz_copied"], 1)
            dve.wait_ge(sem["conv_zeroed"], 1)
            for a in range(2):
                w = c("d_cw")[:, a * CONV:(a + 1) * CONV]
                chain(nc.vector.tensor_scalar(d_c[:, a, :], convbuf[:, a, 0:S], w[:, 0:1], None, ALU.mult))
                for j in range(1, CONV):
                    ins = nc.vector.scalar_tensor_tensor(d_c[:, a, :], convbuf[:, a, j:j + S], w[:, j:j + 1], d_c[:, a, :],
                                                         ALU.mult, ALU.add)
                    if j < CONV - 1:
                        chain(ins)
                ins.then_inc(sem["conv_done"], 1)
            yield "dproj"
            for t in range(NT):
                dve.wait_ge(sem["squares_done"], t + 1)
                chain(nc.vector.tensor_reduce(d_sm[:, 0, t, :], d_sq.rearrange("p (h d) -> p h d", d=DK), AX.X, ALU.add))
                nc.vector.tensor_scalar(d_sm[:, 0, t, :], d_sm[:, 0, t, :], L2_EPS, None, ALU.add).then_inc(sem["sums_in"], 1)
                ins = nc.vector.tensor_tensor(d_sm[:, 1, t, :], bb[1 + t][:, 2 * QK + VD:2 * QK + VD + 2 * HD],
                                              c("d_bias"), ALU.add)
            chain(ins)
            yield "dtok"
            chain(nc.vector.tensor_scalar(d_sm[:, 2], d_sm[:, 1], -1.0, None, ALU.mult))
            nc.vector.tensor_copy(d_sm[:, 3, :, HD:], d_sm[:, 2, :, HD:])
            nc.vector.tensor_tensor(d_sm[:, 3, :, 0:HD], d_sm[:, 1, :, 0:HD], d_sm[:, 2, :, 0:HD], ALU.min).then_inc(sem["gates_in"], 1)
            dve.wait_ge(sem["gates_exp"], 1)
            nc.vector.tensor_scalar(d_sm[:, 3], d_sm[:, 3], 1.0, None, ALU.add).then_inc(sem["gates_one"], 1)
            dve.wait_ge(sem["gates_one"], 1)
            nc.vector.reciprocal(d_sm[:, 4, :, HD:], d_sm[:, 3, :, HD:])
            dve.wait_ge(sem["gates_ln"], 1)
            chain(nc.vector.scalar_tensor_tensor(d_sm[:, 5, :, 0:HD], d_sm[:, 1, :, 0:HD], 0.0, d_sm[:, 4, :, 0:HD],
                                                 ALU.max, ALU.add))
            nc.vector.tensor_tensor(d_sm[:, 5, :, 0:HD], d_sm[:, 5, :, 0:HD],
                                    neg_a[:, :].unsqueeze(1).to_broadcast([P, NT, HD]), ALU.mult).then_inc(sem["gates_ready"], 1)
            for t in range(NT):
                dve.wait_ge(sem["sums_out"], t + 1)
                beta = d_sm[:, 4, t, HD:]
                for part, first in ((0, QK), (1, 0)):
                    ins = nc.vector.tensor_tensor(kqb[:, t, part, :, 0:DK],
                                                  bb[1 + t][:, first:first + QK].rearrange("p (h d) -> p h d", d=DK),
                                                  d_sm[:, 0, t, first // DK:first // DK + HD].unsqueeze(2).to_broadcast([P, HD, DK]),
                                                  ALU.mult)
                chain(ins)
                nc.vector.tensor_tensor(d_r[:, t], bb[1 + t][:, 2 * QK:2 * QK + VD].rearrange("p (h v) -> p h v", v=DV),
                                        beta.unsqueeze(2).to_broadcast([P, HD, DV]), ALU.mult)
                ins = nc.vector.tensor_tensor(kqb[:, t, 2], kqb[:, t, 0], beta.unsqueeze(2).to_broadcast([P, HD, DKP]), ALU.mult)
                ins.then_inc(sem["kqb_ready"], 1)
            yield "dgates"
            for t in range(NT):
                yield "decay"
                dve.wait_ge(sem["decay_ready"], t + 1)
                for h in range(HD):
                    dve.wait_ge(sem["kk_psum"], HD * t + h + 1)
                    nc.vector.tensor_tensor(d_MA[:, h], bb[h][:, 0:2 * P].rearrange("p (a t) -> p a t", a=2),
                                            d_E[:, h, :].unsqueeze(1).to_broadcast([P, 2, P]), ALU.mult).then_inc(sem["ma_ready"], 1)
                yield "kk"
                if t:
                    dve.wait_ge(sem["ks_psum"], 1)
                    dve.wait_ge(sem["cum_exp"], 1)
                    for a in range(2):
                        ins = nc.vector.tensor_tensor(d_t[:, a], bb[3][:, a * VD:(a + 1) * VD].rearrange("p (h v) -> p h v", v=DV),
                                                      d_sm[:, 6, 0, 0:HD].unsqueeze(2).to_broadcast([P, HD, DV]), ALU.mult)
                    chain(ins)
                    nc.vector.tensor_tensor(d_r[:, t], d_r[:, t], d_t[:, 0], ALU.subtract).then_inc(sem["r_ready"], 1)
                else:
                    dve.wait_ge(sem["kqb_ready"], 1)
                y2 = 2 * (LEVELS - 2) + 1
                eye = ident.unsqueeze(1).to_broadcast([P, HD, P])
                psum4 = [b[:, :].rearrange("p (h t) -> p h t", h=HD) for b in bb]
                for l in range(LEVELS):
                    if l == 0:
                        dve.wait_ge(sem["bm_ready"], LEVELS * t + 1)
                        nc.vector.tensor_tensor(d_XT, eye, d_Bm, ALU.subtract)
                        dve.wait_ge(sem["p_psum"], LEVELS * t + 1)
                        nc.vector.tensor_tensor(d_X, eye, psum4[0], ALU.subtract).then_inc(sem["x_updated"], 1)
                    yield "level"
                    if l:
                        if l < LEVELS - 1:
                            dve.wait_ge(sem["y2_psum"], y2 * t + 2 * l - 1)
                            nc.vector.tensor_tensor(d_X, d_X, psum4[1], ALU.subtract)
                        dve.wait_ge(sem["y2_psum"], y2 * t + min(2 * l, y2))
                        dve.wait_ge(sem["x_updated"], LEVELS * t + l)
                        nc.vector.tensor_tensor(d_XT, d_XT, psum4[2], ALU.subtract).then_inc(sem["x_updated"], 1)
                    yield "level2"
                dve.wait_ge(sem["u_psum"], t + 1)
                nc.vector.tensor_copy(d_u.rearrange("p h v -> p (h v)"), bb[0][:, 0:VD]).then_inc(sem["u_ready"], 1)
                yield "u"
                dve.wait_ge(sem["o_psum"], t + 1)
                of = d_o.rearrange("p h v -> p (h v)")
                if t:
                    nc.vector.tensor_tensor(of, bb[1][:, 0:VD], d_t[:, 1].rearrange("p h v -> p (h v)"), ALU.add).then_inc(sem["o_ready"], 1)
                else:
                    nc.vector.tensor_copy(of, bb[1][:, 0:VD]).then_inc(sem["o_ready"], 1)
                    dve.wait_ge(sem["st_psum"], 1)
                    nc.vector.tensor_tensor(d_st, bb[3][:, 0:VD], c("blockmask"), ALU.mult).then_inc(sem["st_ready"], 1)
                dve.wait_ge(sem["o_squared"], t + 1)
                chain(nc.vector.tensor_reduce(d_sm[:, 7, t, 0:HD], d_sq[:, 0:VD].rearrange("p (h v) -> p h v", v=DV), AX.X, ALU.add))
                nc.vector.tensor_scalar(d_sm[:, 7, t, 0:HD], d_sm[:, 7, t, 0:HD], 1.0 / DV, LN_EPS, ALU.mult,
                                        ALU.add).then_inc(sem["sums_in"], 1)
                dve.wait_ge(sem["sums_out"], NT + t + 1)
                chain(nc.vector.tensor_tensor(d_o, d_o, d_sm[:, 7, t, 0:HD].unsqueeze(2).to_broadcast([P, HD, DV]), ALU.mult))
                dve.wait_ge(sem["gate_scaled"], 1)
                nc.vector.tensor_tensor(d_o, d_o, d_gs[:, t], ALU.mult).then_inc(sem["o_gated"], 1)
                yield "o"
                yield "oT"
                dve.wait_ge(sem["layer_psum"], 1 + t)
                nc.vector.tensor_tensor(xb[:, t, :], bb[3][:, 0:P], xb[:, t, :], ALU.add).then_inc(sem["tile_added"], 1)
                yield "dout"
            dve.wait_ge(sem["tile_added"], NT)
            back_norm_dve(dve, chain, 2)
            yield "norm"
            yield "turn"
            dve.wait_ge(sem["pkv_psum"], 1)
            nc.vector.tensor_scalar(p_t[:, 0, :], bb[0][:, 0:S], 0.0, None, ALU.min).then_inc(sem["clipped"], 1)
            dve.wait_ge(sem["pq_psum"], 1)
            nc.vector.tensor_scalar(p_t[:, 1, :], bb[2][:, 0:S], 0.0, None, ALU.min).then_inc(sem["clipped"], 1)
            for a in range(2):
                dve.wait_ge(sem["clipped_exp"], a + 1)
                ins = nc.vector.scalar_tensor_tensor(p_k[:, a, :], bb[2 * a][:, 0:S], 0.0, p_t[:, a, :], ALU.max, ALU.add)
            chain(ins)
            chain(nc.vector.tensor_tensor(p_kv, bb[0][:, S:2 * S], p_k[:, 0, :], ALU.mult))
            one = c("ones")[:, 0:1].to_broadcast([P, S])
            nc.vector.tensor_tensor_scan(p_kp, one, p_k[:, 0, :], 0.0, ALU.mult, ALU.add)
            chain(nc.vector.tensor_tensor_scan(p_vp, one, p_kv, 0.0, ALU.mult, ALU.add))
            nc.vector.reciprocal(p_kp, p_kp)
            chain(nc.vector.tensor_tensor(p_vp, p_vp, p_kv, ALU.add))
            chain(nc.vector.tensor_tensor(p_vp, p_vp, p_kp, ALU.mult))
            nc.vector.tensor_tensor(p_vp, p_vp, p_k[:, 1, :], ALU.mult).then_inc(sem["prefix_done"], 1)
            yield "prefix"
            dve.wait_ge(sem["layer_psum"], 1 + NT)
            chain(nc.vector.tensor_tensor(xf, bb[3][:, 0:S], xf, ALU.add))
            back_norm_dve(dve, chain, 3)
            yield "pout"
            yield "turn"
            dve.wait_ge(sem["logits_psum"], 2)
            chain(nc.vector.tensor_copy(g8[:, 0, :], bb[2][:, 0:NT * E]))
            for t in range(NT):
                ins = nc.vector.max(mx8[:, t, :], g8[:, 0, t * E:(t + 1) * E])
            chain(ins)
            for t in range(NT):
                ins = nc.vector.tensor_scalar(g8[:, 3, t * E:(t + 1) * E], g8[:, 0, t * E:(t + 1) * E], mx8[:, t, 0:1],
                                              None, ALU.subtract)
            ins.then_inc(sem["shifted"], 1)
            dve.wait_ge(sem["shifted_exp"], 2)
            chain(share_dve(chain, g8[:, 5, :], g8[:, 3, :]))
            top2_dve(dve, chain, g8[:, 5, :], 2, 3)
            yield "gate"
            yield "combT"
            dve.wait_ge(sem["b2_psum"], 2)
            dve.wait_ge(sem["xT_psum"], 3)
            chain(nc.vector.tensor_tensor(xf, bb[2][:, 0:S], xf, ALU.add))
            nc.vector.tensor_tensor(xb[:, :, :], xb[:, :, :], c("g_bs2").unsqueeze(1).to_broadcast([P, NT, D]),
                                    ALU.add).then_inc(sem["b2_taken"], 1)
            dve.wait_ge(sem["b2_taken"], 2)
            yield "b2"
            for e in range(E + NSH + 2):
                if e < E + NSH:
                    dve.wait_ge(sem["h1_ready"], e + 1)
                    dve.wait_ge(sem["h3_psum"], e + 1)
                    b3 = c("g_b3") if e < E else c("g_bs3")
                    for kf in range(KF):
                        n = (e if e < E else e - E) * KF + kf
                        ins = nc.vector.scalar_tensor_tensor(h1s[:, e % 2, kf, :], bb[1][:, kf * S:(kf + 1) * S],
                                                             b3[:, n:n + 1], h1s[:, e % 2, kf, :], ALU.add, ALU.mult)
                    ins.then_inc(sem["prod_ready"], 1)
                if e >= 2:
                    add_expert(dve, e - 2, E + e - 2)
                yield "gexpert"
            dve.wait_ge(sem["y_added"], 2 * E + NSH)
            back_norm_dve(dve, chain, 4)
            yield "norm"

        def add_expert(dve, e, count):
            dve.wait_ge(sem["y_psum"], count + 1)
            if count:
                dve.wait_ge(sem["y_added"], count)
            bank = bb[2 + e % 2]
            if e < E:
                for t in range(NT):
                    ins = nc.vector.scalar_tensor_tensor(xb[:, t, :], bank[:, halves(t)], g8[:, 4, t * E + e:t * E + e + 1],
                                                         xb[:, t, :], ALU.mult, ALU.add)
            else:
                xf = xb[:, :, :].rearrange("p t d -> p (t d)")
                ins = nc.vector.tensor_tensor(xf, bank[:, 0:S], xf, ALU.add)
            ins.then_inc(sem["y_added"], 1)

        def back_pool(gps):
            yield "start"
            yield "gate"
            yield "combT"
            yield "b2"
            for e in range(E + 1):
                yield "expert"
            norm_pool(gps, b_mv, "back_var", "back_rstd", 1)
            yield "norm"
            yield "turn"
            gps.wait_ge(sem["normed"], 1)
            nc.gpsimd.memset(convbuf[:, :, 0:1], 0.0)
            nc.gpsimd.memset(convbuf[:, :, S + 1:S + CONV - 1], 0.0).then_inc(sem["conv_zeroed"], 1)
            yield "dproj"
            for t in range(NT):
                gps.wait_ge(sem["sums_in"], t + 1)
                nc.gpsimd.tensor_tensor(d_sm[:, 0, t, :], d_sm[:, 0, t, :], mhalf[:, :], ALU.pow).then_inc(sem["sums_out"], 1)
            yield "dtok"
            gps.wait_ge(sem["gate_silu"], 1)
            nc.gpsimd.tensor_tensor(d_gs.rearrange("p t h v -> p (t h) v"), d_gs.rearrange("p t h v -> p (t h) v"),
                                    c("d_gn").unsqueeze(1).to_broadcast([P, NT * HD, DV]), ALU.mult).then_inc(sem["gate_scaled"], 1)
            yield "dgates"
            for t in range(NT):
                gps.wait_ge(sem["gates_ready"], 1)
                if t:
                    gps.wait_ge(sem["p_psum"], LEVELS * t)
                for h in range(HD):
                    ins = nc.gpsimd.tensor_scalar(d_Bm[:, h, :], c("upper"), d_sm[:, 5, t, h:h + 1], None, ALU.mult)
                ins.then_inc(sem["gm_ready"], 1)
                gps.wait_ge(sem["decay_exp"], t + 1)
                nc.gpsimd.tensor_tensor(d_E, d_E, c("upper").unsqueeze(1).to_broadcast([P, HD, P]), ALU.mult).then_inc(sem["decay_ready"], 1)
                if t == 0:
                    gps.wait_ge(sem["decay_ready"], 1)
                    gps.wait_ge(sem["kqb_ready"], 1)
                    nc.gpsimd.tensor_tensor(d_kh, kqb[:, t, 0], d_E[:, :, P - 1].unsqueeze(2).to_broadcast([P, HD, DKP]),
                                            ALU.mult).then_inc(sem["kh_ready"], 1)
                yield "decay"
                yield "kk"
                for l in range(LEVELS):
                    if l == 0:
                        gps.wait_ge(sem["ma_ready"], HD * (t + 1))
                        gps.wait_ge(sem["decay_psum"], t + 1)
                    else:
                        gps.wait_ge(sem["p_psum"], LEVELS * t + l)
                        if l == 1:
                            gps.wait_ge(sem["x_updated"], LEVELS * t + 1)
                    nc.gpsimd.tensor_tensor(d_Bm, d_MA[:, :, 1, :], c("levels")[:, halves(l)].unsqueeze(1).to_broadcast([P, HD, P]),
                                            ALU.mult).then_inc(sem["bm_ready"], 1)
                    yield "level"
                    yield "level2"
                yield "u"
                gps.wait_ge(sem["sums_in"], NT + t + 1)
                nc.gpsimd.tensor_tensor(d_sm[:, 7, t, 0:HD], d_sm[:, 7, t, 0:HD], mhalf[:, 0:HD], ALU.pow).then_inc(sem["sums_out"], 1)
                yield "o"
                yield "oT"
                yield "dout"
            norm_pool(gps, b_mv, "back_var", "back_rstd", 2)
            yield "norm"
            yield "turn"
            yield "prefix"
            norm_pool(gps, b_mv, "back_var", "back_rstd", 3)
            yield "pout"
            yield "turn"
            yield "gate"
            yield "combT"
            yield "b2"
            for e in range(E + NSH + 2):
                yield "gexpert"
            norm_pool(gps, b_mv, "back_var", "back_rstd", 4)
            yield "norm"

        def alternate(front, back):
            done_f = done_b = 0
            nf, nb = len(SLOTS["front"]), len(SLOTS["back"])
            while done_f < (nf if front else 0) or done_b < (nb if back else 0):
                f_next = front is not None and done_f < nf and (back is None or done_b >= nb or done_f * nb <= done_b * nf)
                if f_next:
                    label = next(front)
                    assert label == SLOTS["front"][done_f], (label, done_f)
                    done_f += 1
                else:
                    label = next(back)
                    assert label == SLOTS["back"][done_b], (label, done_b, SLOTS["back"][done_b])
                    done_b += 1
            for g in (front, back):
                assert g is None or next(g, None) is None

        SLOTS = {"front": [u[0] for u in uses] + ["norm", "xstart", "xproj"] + ["head"] * (HX + 3) + ["xout"]}
        head = ["start", "gate", "combT", "b2"]
        tile_slots = ["decay", "kk"] + ["level", "level2"] * LEVELS + ["u", "o", "oT", "dout"]
        SLOTS["back"] = (head + ["expert"] * (E + 1) + ["norm", "turn", "dproj", "dtok", "dgates"] + tile_slots * NT
                         + ["norm", "turn", "prefix", "pout", "turn", "gate", "combT", "b2"]
                         + ["gexpert"] * (E + NSH + 2) + ["norm"])

        def clear():
            with nc.Block() as block:
                @block.gpsimd
                def _(gps):
                    for n in names:
                        gps.sem_clear(sem[n])

        def chained(eng, name):
            count = [0]

            def chain(ins):
                count[0] += 1
                ins.then_inc(sem[name], 1)
                eng.wait_ge(sem[name], count[0])
            return chain

        def batches(front, back):
            with nc.Block() as block:
                @block.sync
                def _(sp):
                    if front is not None:
                        sp.dma_start(x_in[:, :, :], x[front].rearrange("(t p) d -> p t d", p=P)).then_inc(sem["x_loaded"], 16)
                        sp.dma_start(a_ctx[:, :, :], ctx[front].rearrange("(t p) d -> p t d", p=P)).then_inc(sem["a_ctx_loaded"], 16)
                    if back is not None:
                        sp.dma_start(ctx_in[:, :, :], ctx[back].rearrange("(t p) d -> p t d", p=P)).then_inc(sem["ctx_loaded"], 16)
                        sp.wait_ge(sem["normed"], 4)
                        sp.dma_start(out[back].rearrange("(t p) d -> p t d", p=P), xb[:, :, :]).then_inc(sem["stored"], 16)
                        sp.wait_ge(sem["stored"], 16)

                @block.tensor
                def _(pe):
                    alternate(front_pe(pe) if front is not None else None, back_pe(pe) if back is not None else None)

                @block.scalar
                def _(act):
                    alternate(front_act(act) if front is not None else None, back_act(act) if back is not None else None)

                @block.vector
                def _(dve):
                    chain = chained(dve, "dve_chain")
                    alternate(front_dve(dve, chain, back is not None) if front is not None else None,
                              back_dve(dve, chain) if back is not None else None)

                @block.gpsimd
                def _(gps):
                    alternate(front_pool(gps) if front is not None else None, back_pool(gps) if back is not None else None)
            clear()

        with nc.Block() as block:
            @block.sync
            def _(sp):
                sp.dma_start(small_sb[:, :], small).then_inc(sem["weights_loaded"], 16)
                sp.dma_start(wqkv_sb[:, :, :], w_qkv.rearrange("p (w n) -> p w n", w=3)).then_inc(sem["x_loaded"], 16)
                sp.dma_start(wo_sb[:, :, :], w_o.rearrange("p (j n) -> p j n", n=P)).then_inc(sem["x_loaded"], 16)
                sp.dma_start(f_sb[:, :, :], f_w.rearrange("p (w n) -> p w n", w=2)).then_inc(sem["x_loaded"], 16)
                sp.dma_start(g_sb[:, :, :], g_w.rearrange("p (w n) -> p w n", w=3)).then_inc(sem["x_loaded"], 16)
                sp.wait_ge(sem["x_loaded"], 64)

            @block.tensor
            def _(pe):
                pe.wait_ge(sem["weights_loaded"], 16)
                nc.tensor.matmul(bb[0][:, 0:P], c("d_wsoT")[:, 0:P], c("d_wtop"), start=True, stop=True)
                nc.tensor.matmul(bb[0][0:VD - P, P:2 * P], c("d_wsoT")[:, P:VD], c("d_wtop"), start=True,
                                 stop=True).then_inc(sem["wd_psum"], 1)

            @block.scalar
            def _(act):
                act.wait_ge(sem["weights_loaded"], 16)
                nc.scalar.activation(neg_a[:, :], c("d_alog"), ACT.Exp).then_inc(sem["alog_exp"], 1)

            @block.vector
            def _(dve):
                nc.vector.memset(mhalf[:, :], -0.5)
                nc.vector.memset(rep8[:, :, :], BIG)
                nc.vector.memset(kqb[:, :, :, :, :].rearrange("p a b c d -> p (a b c d)"), 0.0)
                dve.wait_ge(sem["alog_exp"], 1)
                nc.vector.tensor_scalar(neg_a[:, :], neg_a[:, :], -1.0, None, ALU.mult)
                dve.wait_ge(sem["wd_psum"], 1)
                nc.vector.tensor_copy(wd_sb[:, 0, :], bb[0][:, 0:P])
                nc.vector.tensor_copy(wd_sb[0:VD - P, 1, :], bb[0][0:VD - P, P:2 * P])
        clear()

        batches(0, None)
        with nc.Fori(1, B) as i:
            batches(i, i - 1)
        batches(None, B - 1)


def layouts(a):
    import numpy as np

    def rows(v):
        return np.broadcast_to(np.asarray(v).reshape(1, -1), (P, np.asarray(v).size))

    def cols(v):
        return np.asarray(v).reshape(-1, P).T

    def top(v):
        v = np.asarray(v)
        return np.concatenate([v, np.zeros((P - v.shape[0], v.shape[1]), v.dtype)], 0)

    p = np.arange(P)
    upper = (p[:, None] <= p[None, :]).astype(np.float32)
    strict = (p[:, None] > p[None, :]).astype(np.float32)
    levels = []
    for l in range(LEVELS):
        same = (p[:, None] >> (l + 1)) == (p[None, :] >> (l + 1))
        levels.append((same & ((p[:, None] >> l) % 2 == 0) & ((p[None, :] >> l) % 2 == 1)).astype(np.float32))
    block = np.zeros((P, HD, DV), np.float32)
    for h in range(HD):
        block[h * DKP:(h + 1) * DKP, h] = 1
    g = a.get
    conv = np.concatenate([g("L1_attn_conv_x_w")[:, 0, :], g("L1_attn_conv_z_w")[:, 0, :]], 1)
    parts = {
        "ident": np.eye(P, dtype=np.float32), "upper": upper, "strict": strict, "levels": np.concatenate(levels, 1),
        "headmask": (p[:, None] // DX == np.arange(HX)[None, :]).astype(np.float32),
        "fold": (p[:, None] % HALF == p[None, :] % HALF).astype(np.float32),
        "blockmask": block.reshape(P, VD), "ones": np.ones((P, P), np.float32), "bo": rows(g("L0_attn_bo")),
        "x_wq": g("L0_xattn_wq_w").T, "x_wk": g("L0_xattn_wk_w").T, "x_wv": g("L0_xattn_wv_w").T, "x_wo": g("L0_xattn_wo_w").T,
        "x_bq": cols(g("L0_xattn_wq_b")), "x_bk": cols(g("L0_xattn_wk_b")), "x_bv": rows(g("L0_xattn_wv_b")),
        "x_bo": rows(g("L0_xattn_wo_b")),
        "f_b1": cols(g("L0_ffn_b1")), "f_b2": top(g("L0_ffn_b2")), "f_wg": g("L0_ffn_Wg").T, "f_bg": rows(g("L0_ffn_bg")),
        "d_win": g("L1_attn_W_in"), "d_cw": conv,
        "d_cb": np.stack([g("L1_attn_conv_x_b"), g("L1_attn_conv_z_b")], 1),
        "d_wqkv": np.concatenate([g("L1_attn_W_q"), g("L1_attn_W_k"), g("L1_attn_W_v"), g("L1_attn_W_gk"), g("L1_attn_W_b")], 1),
        "d_wg": g("L1_attn_W_g"), "d_bias": rows(np.concatenate([g("L1_attn_dt_bias"), g("L1_attn_b_b")])),
        "d_alog": rows(g("L1_attn_A_log")), "d_gn": rows(g("L1_attn_g_norm_w")), "d_wsoT": g("L1_attn_W_so").T,
        "d_wtop": g("L1_attn_W_out")[0:P], "d_wbot": g("L1_attn_W_out")[P:2 * P],
        "p_wq": g("L1_xattn_Wq").T, "p_wk": g("L1_xattn_Wk").T, "p_wv": g("L1_xattn_Wv").T,
        "g_b1": cols(g("L1_ffn_b1")), "g_b3": cols(g("L1_ffn_b3")), "g_b2": top(g("L1_ffn_b2")), "g_wg": g("L1_ffn_Wg"),
        "g_bs1": cols(g("L1_ffn_bs1")), "g_bs3": cols(g("L1_ffn_bs3")), "g_bs2": rows(g("L1_ffn_bs2")),
    }
    assert all(parts[n].shape == (P, k) for n, k in SMALL), [(n, parts[n].shape, k) for n, k in SMALL if parts[n].shape != (P, k)]
    wo = g("L0_attn_Wo").reshape(HA, 2, HA // 2, D).transpose(1, 0, 2, 3).reshape(P, -1)

    def up(w, shared=None):
        w = w.transpose(1, 0, 2).reshape(D, -1)
        return w if shared is None else np.concatenate([w, shared], 1)

    def down(w, shared=None):
        w = w.reshape(-1, D)
        w = w if shared is None else np.concatenate([w, shared], 0)
        return w.reshape(-1, P, D).transpose(1, 0, 2).reshape(P, -1)

    return {
        "x": g("x"), "ctx": g("ctx_1024"),
        "small": np.concatenate([parts[n] for n, _ in SMALL], 1),
        "w_qkv": np.concatenate([g("L0_attn_Wq"), g("L0_attn_Wk"), g("L0_attn_Wv")], 1), "w_o": wo,
        "f_w": np.concatenate([up(g("L0_ffn_W1").transpose(0, 2, 1)), down(g("L0_ffn_W2").transpose(0, 2, 1))], 1),
        "g_w": np.concatenate([up(g("L1_ffn_W1"), g("L1_ffn_Ws1")), up(g("L1_ffn_W3"), g("L1_ffn_Ws3")),
                               down(g("L1_ffn_W2"), g("L1_ffn_Ws2"))], 1),
    }


def kernel(**inputs):
    import numpy as np
    import concourse.bacc as bacc
    from concourse.bass_utils import run_bass_kernel_spmd

    nc = bacc.Bacc("TRN2", target_bir_lowering=False, num_devices=1)
    arrays, args = {}, []
    for name, a in layouts({k: np.asarray(v) for k, v in inputs.items()}).items():
        a = np.ascontiguousarray(a)
        arrays[f"in_{name}"] = a
        args.append(nc.dram_tensor(f"in_{name}", a.shape, mybir.dt.from_np(a.dtype), kind="ExternalInput").ap())
    args.append(nc.dram_tensor("out", (B, S, D), F32, kind="ExternalOutput").ap())
    build(nc, *args)
    r = run_bass_kernel_spmd(nc, [arrays], core_ids=[0])
    return r.results[0]["out"]
```

```python
from contextlib import ExitStack

import concourse.bass as bass
from concourse import mybir

F32 = mybir.dt.float32
ALU = mybir.AluOpType
ACT = mybir.ActivationFunctionType
AX = mybir.AxisListType

P = 128
B, S, D = 8, 256, 128
NT = S // P
HA = 64
HALF = P // 2
HX, DX = 16, 8
E = 8
FF = 256
KF = FF // P
NSH = 2
HD, DK, DV = 4, 24, 48
DKP = 32
QK, VD = HD * DK, HD * DV
CONV = 4
LEVELS = 7
GP = 3
WO_SLOTS = 4
LN_EPS, ATT_EPS, L2_EPS = 1e-5, 1e-6, 1e-6
BIG = 3e38

SMALL = [
    ("ident", P), ("upper", P), ("strict", P), ("levels", LEVELS * P), ("headmask", HX), ("blockmask", VD),
    ("fold", P),
    ("ones", P), ("bo", P),
    ("x_wq", P), ("x_wk", P), ("x_wv", P), ("x_wo", P), ("x_bq", 1), ("x_bk", 1), ("x_bv", P), ("x_bo", P),
    ("f_b1", E * KF), ("f_b2", P), ("f_wg", E), ("f_bg", E),
    ("d_win", 2 * P), ("d_cw", 2 * CONV), ("d_cb", 2), ("d_wqkv", 2 * QK + VD + 2 * HD), ("d_wg", VD),
    ("d_bias", 2 * HD), ("d_alog", HD), ("d_gn", DV), ("d_wsoT", VD), ("d_wtop", P), ("d_wbot", P),
    ("p_wq", P), ("p_wk", P), ("p_wv", P),
    ("g_b1", E * KF), ("g_b3", E * KF), ("g_b2", P), ("g_wg", E), ("g_bs1", NSH * KF), ("g_bs3", NSH * KF),
    ("g_bs2", P),
]
AT = {}
_at = 0
for _name, _n in SMALL:
    AT[_name] = (_at, _n)
    _at += _n
NSMALL = _at


GATE_SLOTS = {1: ["gate", "gate2"], 2: ["gate", "gate2", "gate3"]}
TURNS = (
    1, 1, 2, 1, 4, 1, 2, 1, 3, 1, 3, 1, 2, 1, 3, 1, 6, 1, 2, 1, 2, 1, 2, 1, 2, 1, 2, 1, 1, 2, 1, 1, 1, 2, 1, 2, 3,
    2, 6, 4, 4, 1, 2, 1, 5, 1, 5, 2, 1, 1, 1, 1, 1, 1, 1, 1, 2, 1, 2, 1, 1, 1, 1, 1, 1, 1, 1, 2, 1, 1, 1, 3, 2, 1,
    1, 3, 2, 1, 1, 1, 2, 2, 1, 1, 1, 8, 1, 2, 1, 1, 1, 1, 1, 1, 1, 1, 1, 1, 1, 2, 1, 1, 1, 4, 1, 1, 1, 1, 1, 2, 1,
    2, 1, 14, 1, 2, 1,
)


def groups():
    out = []
    for first in range(0, HALF // 2, GP):
        for half in range(2):
            out.append((half, first, min(GP, HALF // 2 - first)))
    return out


def build(nc, x, ctx, small, w_qkv, w_o, f_w, g_w, out):
    G = groups()
    NG = len(G)
    with ExitStack() as stack:
        def sb(name, shape):
            return stack.enter_context(nc.sbuf_tensor(name, shape, F32))

        small_sb = sb("small_sb", [P, NSMALL])
        wqkv_sb = sb("wqkv_sb", [P, 3, HA * HA])
        wo_sb = sb("wo_sb", [P, HA // 2, P])
        f_sb = sb("f_sb", [P, 2, E * FF])
        g_sb = sb("g_sb", [P, 3, (E + NSH) * FF])
        wd_sb = sb("wd_sb", [P, 2, P])
        neg_a = sb("neg_a", [P, HD])
        mhalf = sb("mhalf", [P, 8])

        def c(name, rows=P):
            a, n = AT[name]
            return small_sb[0:rows, a:a + n]

        ident = c("ident")
        x_in = sb("x_in", [P, NT, D])
        x_inT = sb("x_inT", [P, S])
        q_sb = sb("q_sb", [P, HALF, HA])
        v_sb = sb("v_sb", [P, HALF // 2, 2 * HA + 1])
        kacc = q_sb[:, 0:8, :].rearrange("p (a b) i -> p a (b i)", a=4)
        ksum = sb("ksum", [P, P])
        rnorm = sb("rnorm", [P, 2, 2, GP])
        handoff = sb("handoff", [P, NT, D])
        f_stat = sb("f_stat", [P, NT, 6])
        f_mv = sb("f_mv", [P, NT, 2])
        ctx_in = sb("ctx_in", [P, NT, D])
        a_ctx = sb("a_ctx", [P, NT, D])
        cxT = sb("cxT", [P, 2, S])
        ctxT, xT = cxT[:, 0, :], cxT[:, 1, :]
        xb = sb("xb", [P, NT, D])
        b_stat = sb("b_stat", [P, NT, 6])
        b_mv = sb("b_mv", [P, NT, 2])
        kqb = sb("kqb", [P, NT, 3, HD, DKP])
        pool = sb("pool", [P, 6528])
        g8 = sb("g8", [P, 8, NT * E])
        rep8 = sb("rep8", [P, NT, 8])
        mx8 = sb("mx8", [P, NT, 8])
        combT = sb("combT", [E, S])

        used = [0]

        def region(*shape, start=None):
            if start is not None:
                used[0] = start
            n = 1
            for k in shape:
                n *= k
            a = pool[:, used[0]:used[0] + n]
            used[0] += n
            assert used[0] <= 6528, used
            if len(shape) == 1:
                return a
            names = "abcde"[:len(shape)]
            kw = {names[i]: shape[i] for i in range(len(shape))}
            return a.rearrange(f"p ({' '.join(names)}) -> p {' '.join(names)}", **kw)

        vm = q_sb[:, :, :].rearrange("p a b -> p (a b)").rearrange("p (t h c) -> p t h c", t=NT, h=HX)
        v_flat = v_sb[:, :, :].rearrange("p a b -> p (a b)")

        def parts_of_v(first, n):
            return v_flat[:, first * S:(first + n) * S]

        qm = parts_of_v(0, 2).rearrange("p (a s) -> p a s", a=2)
        pr = parts_of_v(2, 4).rearrange("p (a t s) -> p a t s", a=2, t=NT)
        pT = parts_of_v(6, 4).rearrange("p (a t s) -> p a t s", a=2, t=NT)
        kT, qT = parts_of_v(10, 1), parts_of_v(11, 1)
        oT = qT
        a_cxT = parts_of_v(12, 2).rearrange("p (a s) -> p a s", a=2)
        nmax = sb("nmax", [P, 2, NT])
        psum_ = sb("psum_", [P, 2, NT])
        prec = sb("prec", [P, 2, NT])
        hs = region(2, KF, S, start=0)
        h1s = region(2, KF, S)
        d_c = region(2, S, start=0)
        d_s = region(2, S)
        d_E = region(HD, P)
        d_MA = region(HD, 2, P)
        d_Bm = region(HD, P)
        d_X = region(2, 2, HD // 2, P)
        d_P = region(HD, P)
        d_kh = region(HD, DKP)
        d_o = region(HD, DV)
        d_sq = region(NT * 2 * QK)
        d_t = region(2, HD, DV)
        d_oT = d_X.rearrange("p g a h s -> p (g a h s)")[:, 0:2 * P].rearrange("p (a b) -> p a b", a=2)
        d_sm = sb("d_sm", [P, 8, NT, 8])
        side = sb("side", [P, 1536])
        convbuf = side[:, 0:2 * (S + CONV - 1)].rearrange("p (a b) -> p a b", a=2)
        d_kqT = side[:, 0:3 * P].rearrange("p (a b) -> p a b", a=3)
        d_r = side[:, 384:768].rearrange("p (t h v) -> p t h v", t=NT, h=HD)
        d_gs = side[:, 768:1152].rearrange("p (t h v) -> p t h v", t=NT, h=HD)
        d_u = side[:, 1152:1344].rearrange("p (h v) -> p h v", h=HD)
        d_st = side[:, 1344:1536]
        p_k = region(2, S, start=0)
        p_t = region(2, S)
        p_kv = region(S)
        p_kp = region(S)
        p_vp = region(S)

        fb = [stack.enter_context(nc.psum_tensor(f"front{i}", [P, 512], F32)) for i in range(4)]
        bb = [stack.enter_context(nc.psum_tensor(f"back{i}", [P, 512], F32)) for i in range(4)]


        names = """weights_loaded x_loaded ctx_loaded wd_psum alog_exp
            front_filled front_act_drained front_dve_drained front_biased front_var front_rstd front_done
            dve_chain cT_psum
            x1T_psum a_cxT_ready a_ctx_loaded x1_biased xo_psum cxT_psum cxT_ready vm_zeroed xkq_psum xv_psum xkq_ready xv_ready
            qm_ready scores_ready nmax_ready exp_done sums_inverted probs_ready pT_psum pT_ready pv_done
            oT_ready layer_psum back_var back_rstd normed xT_psum xT_ready
            logits_psum shifted shifted_exp comb_ready combT_psum combT_ready b2_psum b2_taken
            h_psum h_ready y_psum y_added tile_added
            xz_psum conv_zeroed xz_copied conv_done silu_done kqv_psum g_psum squares_done sums_in sums_out
            gates_in gates_exp gates_one gates_ln gates_ready kqb_ready kqT_psum kqT_ready gm_ready decay_psum
            decay_exp decay_ready cum_psum cum_exp kk_psum ma_ready bm_ready p_psum p_copied y2_psum x_updated
            kh_ready r_ready u_psum u_ready o_psum o_ready st_psum st_ready ks_psum gate_silu gate_scaled o_squared
            o_gated oTd_psum oTd_ready
            pkv_psum pq_psum clipped clipped_exp prefix_done
            h3_psum h1_ready prod_ready""".split()
        sem = {n: stack.enter_context(nc.semaphore(n)) for n in names}
        lasting = {n: stack.enter_context(nc.semaphore(n)) for n in ("qv_loaded", "wo_loaded", "experts_loaded", "stored")}
        numbers = [sem[n].num for n in names]
        assert numbers == list(range(numbers[0], numbers[0] + len(names)))

        uses = [("xT",)]
        for tile in range(NT):
            uses += [("k", tile, 1, m) for m in range(HA // 8)] + [("ksum", tile)]
            uses += [(kind, tile, w, m) for m in range(HA // 8) for kind, w in (("q", 0), ("v", 2))]
            uses += [("out", tile, half, first, n) for half, first, n in G]
            uses += [("wo", tile)]

        def ends_slot(use):
            return use[0] != "out" or use[2] == 1

        def earlier_slots(use):
            for _ in range(WO_SLOTS - 1 if use[0] == "wo" else 0):
                yield use[0]

        act_drains = [0]
        dve_drains = [0]
        for u in uses:
            act_drains.append(act_drains[-1] + (u[0] == "v"))
            dve_drains.append(dve_drains[-1] + (u[0] != "v"))

        q_pairs = q_sb[:, :, :].rearrange("p (r k) i -> p r (k i)", k=2)

        def front_pe(pe, first_batch):
            for n, use in enumerate(uses):
                kind, bank = use[0], fb[n % 4]
                if n >= 4:
                    last = n - 4
                    if uses[last][0] == "v":
                        pe.wait_ge(sem["front_act_drained"], act_drains[last + 1])
                    else:
                        pe.wait_ge(sem["front_dve_drained"], dve_drains[last + 1])
                if kind == "xT":
                    for t in range(NT):
                        mm = nc.tensor.transpose(bank[:, t * P:(t + 1) * P], x_in[:, t, :], ident)
                elif kind in ("q", "k", "v"):
                    _, tile, w, m = use
                    if n == 1:
                        pe.wait_ge(sem["front_dve_drained"], 1)
                    if first_batch and kind == "q" and tile == m == 0:
                        pe.wait_ge(lasting["qv_loaded"], 32)
                    for k in range(4):
                        mm = nc.tensor.matmul(bank[:, k * P:(k + 1) * P], wqkv_sb[:, w, (4 * m + k) * P:(4 * m + k + 1) * P],
                                              x_inT[:, tile * P:(tile + 1) * P], start=True, stop=True)
                elif kind == "ksum":
                    pe.wait_ge(sem["front_dve_drained"], dve_drains[n])
                    for k in range(4):
                        mm = nc.tensor.matmul(bank[:, 0:P], c("fold"), kacc[:, k, :], start=(k == 0), stop=(k == 3))
                elif kind == "out":
                    _, tile, half, first, count = use
                    if first == 0 and half == 0:
                        pe.wait_ge(sem["front_act_drained"], act_drains[n])
                        pe.wait_ge(sem["front_dve_drained"], dve_drains[n])
                    if half == 0:
                        continue
                    w = 2 * HA + 1
                    for k in range(count):
                        for h in range(2):
                            rows = slice(h * HALF, (h + 1) * HALF)
                            mm = nc.tensor.matmul(fb[(n - 1 + h) % 4][:, k * w:(k + 1) * w], q_pairs[rows, first + k, :],
                                                  v_sb[rows, first + k, :], start=True, stop=True)
                            if h == 0 and k == count - 1:
                                mm.then_inc(sem["front_filled"], 1)
                else:
                    pe.wait_ge(sem["front_dve_drained"], dve_drains[n])
                    if first_batch:
                        pe.wait_ge(lasting["wo_loaded"], 16)
                    for j in range(HA // 2):
                        o = q_sb[:, :, :].rearrange("p t (s j) -> p (t s) j", s=2)[:, :, j]
                        mm = nc.tensor.matmul(bank[:, 0:P], o, wo_sb[:, j, :], start=(j == 0), stop=(j == HA // 2 - 1))
                        if (j + 1) % (HA // 2 // WO_SLOTS) == 0 and j + 1 < HA // 2:
                            yield kind
                mm.then_inc(sem["front_filled"], 1)
                if ends_slot(use):
                    yield kind
            yield "norm"
            yield "norm2"
            yield from cross_pe(pe)

        def cross_pe(pe):
            pe.wait_ge(sem["front_done"], 1)
            for t in range(NT):
                nc.tensor.transpose(fb[0][:, halves(t)], a_ctx[:, t, :], ident)
            for t in range(NT):
                mm = nc.tensor.transpose(fb[0][:, halves(NT + t)], handoff[:, t, :], ident)
            mm.then_inc(sem["x1T_psum"], 1)
            yield "xstart"
            pe.wait_ge(sem["a_cxT_ready"], 1)
            nc.tensor.matmul(fb[1][:, 0:S], c("x_wk"), a_cxT[:, 0, :], start=True, stop=True)
            nc.tensor.matmul(fb[1][:, S:2 * S], c("x_wq"), a_cxT[:, 1, :], start=True, stop=True).then_inc(sem["xkq_psum"], 1)
            for t in range(NT):
                mm = nc.tensor.matmul(fb[2][:, halves(t)], a_cxT[:, 0, halves(t)], c("x_wv"), start=True, stop=True)
            mm.then_inc(sem["xv_psum"], 1)
            yield "xproj"
            for k in range(HX + 3):
                if k < HX:
                    pe.wait_ge(sem["xkq_ready"], 1)
                    pe.wait_ge(sem["qm_ready"], k + 1)
                    if k >= 2:
                        pe.wait_ge(sem["exp_done"], k - 1)
                    for t in range(NT):
                        mm = nc.tensor.matmul(fb[k % 2][:, t * S:(t + 1) * S], qm[:, k % 2, halves(t)], kT,
                                              start=True, stop=True)
                    mm.then_inc(sem["scores_ready"], 1)
                if 0 <= k - 2 < HX:
                    j = k - 2
                    pe.wait_ge(sem["probs_ready"], j + 1)
                    pe.wait_ge(sem["xv_ready"], 1)
                    if j:
                        pe.wait_ge(sem["pT_ready"], j)
                    for st in range(NT):
                        for t in range(NT):
                            mm = nc.tensor.transpose(fb[2][:, st * S + t * P:st * S + (t + 1) * P],
                                                     pr[:, j % 2, t, halves(st)], ident)
                    mm.then_inc(sem["pT_psum"], 1)
                if k >= 3:
                    j = k - 3
                    pe.wait_ge(sem["pT_ready"], j + 1)
                    for st in range(NT):
                        mm = nc.tensor.matmul(fb[3][:, 0:S], vm[:, st, j, :], pT[:, j % 2, st, :],
                                              start=(j == 0 and st == 0), stop=(j == HX - 1 and st == NT - 1))
                    mm.then_inc(sem["pv_done"], 1)
                yield "head"
            pe.wait_ge(sem["oT_ready"], 1)
            for t in range(NT):
                mm = nc.tensor.matmul(fb[0][:, halves(t)], oT[:, halves(t)], c("x_wo"), start=True, stop=True)
            mm.then_inc(sem["xo_psum"], 1)
            yield "xout"

        def front_act(act):
            for n, use in enumerate(uses):
                kind, bank = use[0], fb[n % 4]
                yield from earlier_slots(use)
                if kind == "v":
                    _, tile, w, m = use
                    act.wait_ge(sem["front_filled"], n + 1)
                    for half in range(2):
                        for odd in range(2):
                            src = bank[odd * HALF:(odd + 1) * HALF, :].rearrange("p (m t s) -> p s m t", m=4, s=2)[:, half]
                            dst = v_sb[half * HALF:(half + 1) * HALF, :, 0:2 * HA].rearrange(
                                "p r (k i) -> p r k i", k=2)[:, :, :, 8 * m + odd:8 * m + 8:2].rearrange("p r k m -> p m r k")
                            ins = nc.scalar.activation(dst, src.rearrange("p m (r k) -> p m r k", k=2), ACT.Copy)
                    ins.then_inc(sem["front_act_drained"], 1)
                if ends_slot(use):
                    yield kind
            yield "norm"
            yield "norm2"
            yield from cross_act(act)

        def cross_act(act):
            yield "xstart"
            act.wait_ge(sem["xkq_psum"], 1)
            nc.scalar.activation(kT, fb[1][:, 0:S], ACT.Identity, bias=c("x_bk"))
            nc.scalar.activation(qT, fb[1][:, S:2 * S], ACT.Identity, bias=c("x_bq")).then_inc(sem["xkq_ready"], 1)
            yield "xproj"
            for k in range(HX + 3):
                if k < HX:
                    act.wait_ge(sem["nmax_ready"], k + 1)
                    if k >= 2:
                        act.wait_ge(sem["pT_psum"], k - 1)
                        act.wait_ge(sem["sums_inverted"], k - 1)
                    for t in range(NT):
                        ins = nc.scalar.activation(pr[:, k % 2, t, :], fb[k % 2][:, t * S:(t + 1) * S], ACT.Exp,
                                                   bias=nmax[:, k % 2, t:t + 1], scale=DX ** -0.5,
                                                   accum_out=psum_[:, k % 2, t:t + 1])
                    ins.then_inc(sem["exp_done"], 1)
                yield "head"
            act.wait_ge(sem["pv_done"], HX)
            nc.scalar.activation(oT, fb[3][:, 0:S], ACT.Copy).then_inc(sem["oT_ready"], 1)
            yield "xout"

        def stats_dve(chain, tile_, stat, mv, var):
            for t in range(NT):
                ins = nc.vector.bn_stats(stat[:, t, :], tile_[:, t, :])
            chain(ins)
            for t in range(NT):
                ins = nc.vector.bn_aggr(mv[:, t, :], stat[:, t, :])
            chain(ins)
            nc.vector.tensor_scalar(mv[:, :, 1], mv[:, :, 1], LN_EPS, None, ALU.add).then_inc(sem[var], 1)

        def norm_dve(dve, dst, tile_, mv, rstd, count):
            dve.wait_ge(sem[rstd], count)
            for t in range(NT):
                ins = nc.vector.tensor_scalar(dst[:, t, :], tile_[:, t, :], mv[:, t, 0:1], mv[:, t, 1:2],
                                              ALU.subtract, ALU.mult)
            return ins

        def norm_pool(gps, mv, var, rstd, count):
            gps.wait_ge(sem[var], count)
            nc.gpsimd.tensor_tensor(mv[:, :, 1], mv[:, :, 1], mhalf[:, 0:NT], ALU.pow).then_inc(sem[rstd], 1)

        def front_dve(dve, chain, back_too):
            for n, use in enumerate(uses):
                kind, bank = use[0], fb[n % 4]
                yield from earlier_slots(use)
                if kind == "v":
                    yield kind
                    continue
                dve.wait_ge(sem["front_filled"], n + 1)
                if kind == "xT":
                    ins = nc.vector.tensor_copy(x_inT[:, :], bank[:, 0:S])
                elif kind == "k":
                    m = use[3]
                    if n == 1:
                        nc.vector.memset(v_sb[:, :, 2 * HA:2 * HA + 1], 1.0)
                    acc = kacc.rearrange("p a t -> p (a t)")
                    if m == 0:
                        ins = nc.vector.tensor_scalar(acc, bank[:, :], 0.0, None, ALU.max)
                    else:
                        dve.wait_ge(sem["front_dve_drained"], dve_drains[n])
                        ins = nc.vector.scalar_tensor_tensor(acc, bank[:, :], 0.0, acc, ALU.max, ALU.add)
                elif kind == "ksum":
                    ins = nc.vector.tensor_scalar(ksum[:, :], bank[:, 0:P], HA ** -0.5, None, ALU.mult)
                elif kind == "q":
                    _, tile, w, m = use
                    if m == 0:
                        dve.wait_ge(sem["front_dve_drained"], dve_drains[n])
                    for half in range(2):
                        for odd in range(2):
                            rows = slice(odd * HALF, (odd + 1) * HALF)
                            src = bank[rows, :].rearrange("p (m t s) -> p s m t", m=4, s=2)[:, half]
                            dst = q_sb[half * HALF:(half + 1) * HALF, :, 8 * m + odd:8 * m + 8:2].rearrange("p t m -> p m t")
                            ks = ksum[rows, half::2].unsqueeze(1).to_broadcast([HALF, 4, HALF])
                            ins = nc.vector.scalar_tensor_tensor(dst, src, 0.0, ks, ALU.max, ALU.mult)
                elif kind == "out":
                    _, tile, half, first, count = use
                    if half == 0:
                        continue
                    w = 2 * HA + 1
                    src = [fb[(n - 1 + h) % 4][:, 0:count * w].rearrange("p (r i) -> p r i", i=w) for h in range(2)]
                    rn = rnorm[:, n // 2 % 2, :, 0:count]
                    for h in range(2):
                        ins = nc.vector.tensor_scalar(rn[:, h, :], src[h][:, :, 2 * HA], ATT_EPS, None, ALU.add)
                    chain(ins)
                    chain(nc.vector.reciprocal(rn, rn))
                    for h in range(2):
                        for tok in range(2):
                            for jh in range(2):
                                lo = tok * HALF
                                dst = q_sb[jh * HALF:(jh + 1) * HALF, 2 * first + tok:2 * (first + count) + tok - 1:2,
                                           h * 32:h * 32 + 32]
                                ins = nc.vector.tensor_tensor(
                                    dst, src[h][lo:lo + HALF, :, tok * HA + jh * 32:tok * HA + jh * 32 + 32],
                                    rn[lo:lo + HALF, h, :].unsqueeze(2).to_broadcast([HALF, count, 32]), ALU.mult)
                        if h == 0:
                            ins.then_inc(sem["front_dve_drained"], 1)
                else:
                    if use[1] == 0:
                        dve.wait_ge(sem["front_biased"], 1)
                        if back_too:
                            dve.wait_ge(sem["normed"], 1)
                    ins = nc.vector.tensor_tensor(handoff[:, use[1], :], bank[:, 0:P], x_in[:, use[1], :], ALU.add)
                ins.then_inc(sem["front_dve_drained"], 1)
                if ends_slot(use):
                    yield kind
            dve.wait_ge(sem["front_dve_drained"], dve_drains[-1])
            stats_dve(chain, handoff, f_stat, f_mv, "front_var")
            yield "norm"
            norm_dve(dve, handoff, handoff, f_mv, "front_rstd", 1).then_inc(sem["front_done"], 1)
            yield "norm2"
            yield from cross_dve(dve, chain)

        def cross_dve(dve, chain):
            dve.wait_ge(sem["x1T_psum"], 1)
            nc.vector.tensor_copy(a_cxT.rearrange("p a s -> p (a s)"), fb[0][:, :]).then_inc(sem["a_cxT_ready"], 1)
            nc.vector.tensor_tensor(handoff[:, :, :], handoff[:, :, :], c("x_bo").unsqueeze(1).to_broadcast([P, NT, D]),
                                    ALU.add).then_inc(sem["x1_biased"], 1)
            yield "xstart"
            dve.wait_ge(sem["xv_psum"], 1)
            dve.wait_ge(sem["vm_zeroed"], 1)
            step = P + DX
            for t in range(NT):
                flat = vm[:, t].rearrange("p h c -> p (h c)")
                n = HX - 1
                nc.vector.tensor_tensor(flat[:, 0:n * step].rearrange("p (h c) -> p h c", c=step)[:, :, 0:DX],
                                        fb[2][:, t * P:t * P + n * DX].rearrange("p (h d) -> p h d", d=DX),
                                        c("x_bv")[:, 0:n * DX].rearrange("p (h d) -> p h d", d=DX), ALU.add)
                ins = nc.vector.tensor_tensor(flat[:, n * step:n * step + DX], fb[2][:, t * P + n * DX:(t + 1) * P],
                                              c("x_bv")[:, n * DX:P], ALU.add)
            ins.then_inc(sem["xv_ready"], 1)

            def head_queries(k):
                if k >= 2:
                    dve.wait_ge(sem["scores_ready"], k - 1)
                nc.vector.tensor_scalar(qm[:, k % 2, :], qT, c("headmask")[:, k:k + 1], None, ALU.mult).then_inc(sem["qm_ready"], 1)

            dve.wait_ge(sem["xkq_ready"], 1)
            head_queries(0)
            yield "xproj"
            for k in range(HX + 3):
                if k + 1 < HX:
                    head_queries(k + 1)
                if k < HX:
                    dve.wait_ge(sem["scores_ready"], k + 1)
                    chain(nc.vector.tensor_reduce(nmax[:, k % 2, :], fb[k % 2][:, :].rearrange("p (t s) -> p t s", t=NT),
                                                  AX.X, ALU.max, negate=True))
                    nc.vector.tensor_scalar(nmax[:, k % 2, :], nmax[:, k % 2, :], DX ** -0.5, None,
                                            ALU.mult).then_inc(sem["nmax_ready"], 1)
                if 1 <= k <= HX:
                    j = k - 1
                    dve.wait_ge(sem["exp_done"], j + 1)
                    if j >= 2:
                        dve.wait_ge(sem["probs_ready"], j - 1)
                    nc.vector.reciprocal(prec[:, j % 2, :], psum_[:, j % 2, :]).then_inc(sem["sums_inverted"], 1)
                    dve.wait_ge(sem["sums_inverted"], j + 1)
                    for t in range(NT):
                        ins = nc.vector.tensor_scalar(pr[:, j % 2, t, :], pr[:, j % 2, t, :], prec[:, j % 2, t:t + 1], None, ALU.mult)
                    ins.then_inc(sem["probs_ready"], 1)
                if 0 <= k - 2 < HX:
                    j = k - 2
                    dve.wait_ge(sem["pT_psum"], j + 1)
                    if j >= 2:
                        dve.wait_ge(sem["pv_done"], j - 1)
                    nc.vector.tensor_copy(pT[:, j % 2].rearrange("p a s -> p (a s)"), fb[2][:, :]).then_inc(sem["pT_ready"], 1)
                yield "head"
            dve.wait_ge(sem["xo_psum"], 1)
            dve.wait_ge(sem["x1_biased"], 1)
            x1 = handoff[:, :, :].rearrange("p t d -> p (t d)")
            nc.vector.tensor_tensor(x1, fb[0][:, 0:S], x1, ALU.add)
            yield "xout"

        def front_pool(gps):
            for n, use in enumerate(uses):
                yield from earlier_slots(use)
                if n == 0:
                    gps.wait_ge(sem["front_filled"], 1)
                    nc.gpsimd.tensor_tensor(x_in[:, :, :], x_in[:, :, :],
                                            c("bo").unsqueeze(1).to_broadcast([P, NT, D]), ALU.add).then_inc(sem["front_biased"], 1)
                if ends_slot(use):
                    yield use[0]
            norm_pool(gps, f_mv, "front_var", "front_rstd", 1)
            yield "norm"
            yield "norm2"
            yield from cross_pool(gps)

        def cross_pool(gps):
            gps.wait_ge(sem["front_filled"], len(uses))
            nc.gpsimd.memset(vm.rearrange("p t h c -> p (t h c)"), 0.0).then_inc(sem["vm_zeroed"], 1)
            yield "xstart"

            yield "xproj"
            for k in range(HX + 3):
                yield "head"
            yield "xout"

        def halves(k):
            return slice(k * P, (k + 1) * P)

        def turn_pe(pe, count):
            pe.wait_ge(sem["normed"], count + 1)
            for t in range(NT):
                mm = nc.tensor.transpose(bb[1][:, halves(t)], xb[:, t, :], ident)
            mm.then_inc(sem["xT_psum"], 1)

        def gate_pe(pe, count, wg, b2):
            pe.wait_ge(sem["cxT_ready" if count == 1 else "xT_ready"], 1 if count == 1 else 3)
            for t in range(NT):
                mm = nc.tensor.matmul(bb[2][:, t * E:(t + 1) * E], xT[:, halves(t)], wg, start=True, stop=True)
            mm.then_inc(sem["logits_psum"], 1)
            yield "gate"
            yield from extra_gates(count)
            pe.wait_ge(sem["comb_ready"], count)
            for t in range(NT):
                mm = nc.tensor.transpose(bb[3][0:E, halves(t)], g8[:, 4, t * E:(t + 1) * E], ident)
            mm.then_inc(sem["combT_psum"], 1)
            yield "combT"
            pe.wait_ge(sem["combT_ready"], count)
            for t in range(NT):
                mm = nc.tensor.matmul(bb[2][:, halves(t)], combT[:, halves(t)], b2, start=True, stop=True)
            mm.then_inc(sem["b2_psum"], 1)
            yield "b2"

        def back_pe(pe):
            for t in range(NT):
                mm = nc.tensor.transpose(bb[0][:, halves(t)], ctx_in[:, t, :], ident)
            mm.then_inc(sem["cT_psum"], 1)
            yield "norm"
            yield "norm2"
            pe.wait_ge(sem["normed"], 1)
            for t in range(NT):
                mm = nc.tensor.transpose(bb[0][:, halves(NT + t)], xb[:, t, :], ident)
            mm.then_inc(sem["cxT_psum"], 1)
            yield "start"
            yield from gate_pe(pe, 1, c("f_wg"), c("f_b2", E))
            for e in range(E + 1):
                if e < E:
                    if e >= 2:
                        pe.wait_ge(sem["h_ready"], e - 1)
                    for kf in range(KF):
                        a = e * FF + kf * P
                        mm = nc.tensor.matmul(bb[e % 2][:, kf * S:(kf + 1) * S], f_sb[:, 0, a:a + P], xT,
                                              start=True, stop=True)
                    mm.then_inc(sem["h_psum"], 1)
                if e:
                    j = e - 1
                    pe.wait_ge(sem["h_ready"], j + 1)
                    pe.wait_ge(sem["b2_taken"], 1)
                    if j >= 2:
                        pe.wait_ge(sem["y_added"], j - 1)
                    for t in range(NT):
                        for kf in range(KF):
                            a = (j * KF + kf) * P
                            mm = nc.tensor.matmul(bb[2 + j % 2][:, halves(t)], hs[:, j % 2, kf, halves(t)],
                                                  f_sb[:, 1, a:a + P], start=(kf == 0), stop=(kf == KF - 1))
                    mm.then_inc(sem["y_psum"], 1)
                yield "expert"
            yield "norm"
            yield "norm2"
            turn_pe(pe, 1)
            yield "turn"
            pe.wait_ge(sem["xT_ready"], 1)
            for a in range(2):
                mm = nc.tensor.matmul(bb[0][:, a * S:(a + 1) * S], c("d_win")[:, halves(a)], xT, start=True, stop=True)
            mm.then_inc(sem["xz_psum"], 1)
            yield "dproj"
            yield "conv"
            pe.wait_ge(sem["silu_done"], 1)
            for t in range(NT):
                w = 2 * QK + VD + 2 * HD
                nc.tensor.matmul(bb[1 + t][:, 0:w], d_s[:, 0, halves(t)], c("d_wqkv"), start=True,
                                 stop=True).then_inc(sem["kqv_psum"], 1)
            for t in range(NT):
                mm = nc.tensor.matmul(bb[3][:, t * VD:(t + 1) * VD], d_s[:, 0, halves(t)], c("d_wg"), start=True, stop=True)
            mm.then_inc(sem["g_psum"], 1)
            yield "dtok"
            yield "dtok2"
            yield "dgates"
            yield "dgates2"
            yield "dgates3"
            for t in range(NT):
                yield "gm"
                pe.wait_ge(sem["gm_ready"], t + 1)
                nc.tensor.matmul(bb[0][:, :], c("strict"), d_Bm.rearrange("p h t -> p (h t)"), start=True,
                                 stop=True).then_inc(sem["decay_psum"], 1)
                pe.wait_ge(sem["kqb_ready"], NT)
                for a in range(3):
                    mm = nc.tensor.transpose(bb[1][:, halves(a)], kqb[:, t, a].rearrange("p h d -> p (h d)"), ident)
                mm.then_inc(sem["kqT_psum"], 1)
                if t:
                    nc.tensor.matmul(bb[2][:, 0:HD], c("upper"), d_sm[:, 5, t, 0:HD], start=True,
                                     stop=True).then_inc(sem["cum_psum"], 1)
                yield "decay"
                pe.wait_ge(sem["kqT_ready"], t + 1)
                pe.wait_ge(sem["decay_exp"], t + 1)
                pe.wait_ge(sem["gate_silu"], 1)
                if t:
                    pe.wait_ge(sem["cum_exp"], 1)
                    pe.wait_ge(sem["tile_added"], t)
                for h in range(HD):
                    rows = slice(h * DKP, (h + 1) * DKP)
                    nc.tensor.matmul(bb[h][:, 0:2 * P], d_kqT[rows, 0, :], d_kqT[rows, 1:3, :], start=True,
                                     stop=True).then_inc(sem["kk_psum"], 1)
                yield "kk"
                pe.wait_ge(sem["ma_ready"], HD * (t + 1))
                if t:
                    pe.wait_ge(sem["st_ready"], 1)
                    nc.tensor.matmul(bb[3][:, 0:VD], d_kqT[:, 2, :], d_st, start=True, stop=True)
                    nc.tensor.matmul(bb[3][:, VD:2 * VD], d_kqT[:, 1, :], d_st, start=True,
                                     stop=True).then_inc(sem["ks_psum"], 1)
                for l in range(LEVELS):
                    pe.wait_ge(sem["bm_ready"], LEVELS * t + l + 1)
                    if t and l == 0:
                        pe.wait_ge(sem["r_ready"], 1)
                    for g in range(2):
                        if l:
                            pe.wait_ge(sem["x_updated"], 2 * (LEVELS * t + l - 1) + g + 1)
                        for h in range(HD // 2):
                            mm = nc.tensor.matmul(bb[3 * g][:, halves(h)], d_Bm[:, 2 * g + h, :],
                                                  d_X[:, g, 0, h, :] if l else ident, start=True, stop=True)
                        mm.then_inc(sem["p_psum"], 1)
                    yield "level"
                    if l:
                        for g in range(2):
                            pe.wait_ge(sem["p_copied"], 2 * ((LEVELS - 1) * t + l - 1) + g + 1)
                            for h in range(HD // 2):
                                if l < LEVELS - 1:
                                    nc.tensor.matmul(bb[1 + g][:, halves(h)], d_X[:, g, 1, h, :], d_P[:, 2 * g + h, :],
                                                     start=True, stop=True)
                                mm = nc.tensor.matmul(bb[1 + g][:, halves(2 + h)], d_P[:, 2 * g + h, :], d_X[:, g, 1, h, :],
                                                      start=True, stop=True)
                            mm.then_inc(sem["y2_psum"], 1)
                    yield "level2"
                pe.wait_ge(sem["x_updated"], 2 * LEVELS * (t + 1))
                for h in range(HD):
                    mm = nc.tensor.matmul(bb[0][:, h * DV:(h + 1) * DV], d_X[:, h // 2, 1, h % 2, :], d_r[:, t, h, :], start=True, stop=True)
                mm.then_inc(sem["u_psum"], 1)
                yield "u"
                pe.wait_ge(sem["u_ready"], t + 1)
                for h in range(HD):
                    mm = nc.tensor.matmul(bb[1][:, h * DV:(h + 1) * DV], d_MA[:, h, 0, :], d_u[:, h, :], start=True, stop=True)
                mm.then_inc(sem["o_psum"], 1)
                if t == 0:
                    pe.wait_ge(sem["kh_ready"], 1)
                    nc.tensor.matmul(bb[3][:, 0:VD], d_kh.rearrange("p h d -> p (h d)"), d_u.rearrange("p h v -> p (h v)"),
                                     start=True, stop=True).then_inc(sem["st_psum"], 1)
                yield "o"
                yield "o2"
                yield "o3"
                pe.wait_ge(sem["o_gated"], t + 1)
                of = d_o.rearrange("p h v -> p (h v)")
                nc.tensor.transpose(bb[2][:, 0:P], of[:, 0:P], ident)
                nc.tensor.transpose(bb[2][0:VD - P, P:2 * P], of[:, P:VD], ident).then_inc(sem["oTd_psum"], 1)
                yield "oT"
                pe.wait_ge(sem["oTd_ready"], t + 1)
                if t == 0:
                    pe.wait_ge(sem["st_ready"], 1)
                pe.wait_ge(sem["silu_done"], 2)
                nc.tensor.matmul(bb[3][:, 0:P], d_oT[:, 0, :], wd_sb[:, 0, :], start=True, stop=False)
                nc.tensor.matmul(bb[3][:, 0:P], d_s[:, 1, halves(t)], c("d_wbot"), start=False, stop=False)
                nc.tensor.matmul(bb[3][:, 0:P], d_oT[0:VD - P, 1, :], wd_sb[0:VD - P, 1, :], start=False,
                                 stop=True).then_inc(sem["layer_psum"], 1)
                yield "dout"
            yield "norm"
            yield "norm2"
            turn_pe(pe, 2)
            nc.tensor.matmul(bb[0][:, 0:S], c("p_wk"), ctxT, start=True, stop=True)
            nc.tensor.matmul(bb[0][:, S:2 * S], c("p_wv"), ctxT, start=True, stop=True).then_inc(sem["pkv_psum"], 1)
            yield "turn"
            pe.wait_ge(sem["xT_ready"], 2)
            nc.tensor.matmul(bb[2][:, 0:S], c("p_wq"), xT, start=True, stop=True).then_inc(sem["pq_psum"], 1)
            yield "prefix"
            yield "prefix2"
            yield "prefix3"
            pe.wait_ge(sem["prefix_done"], 1)
            for t in range(NT):
                mm = nc.tensor.transpose(bb[3][:, halves(t)], p_vp[:, halves(t)], ident)
            mm.then_inc(sem["layer_psum"], 1)
            yield "pout"
            yield "norm2"
            turn_pe(pe, 3)
            yield "turn"
            yield from gate_pe(pe, 2, c("g_wg"), c("g_b2", E))
            for e in range(E + NSH + 2):
                if e < E + NSH:
                    if e:
                        pe.wait_ge(sem["h1_ready"], e)
                    for kf in range(KF):
                        a = e * FF + kf * P
                        mm = nc.tensor.matmul(bb[0][:, kf * S:(kf + 1) * S], g_sb[:, 0, a:a + P], xT, start=True, stop=True)
                    mm.then_inc(sem["h_psum"], 1)
                    if e:
                        pe.wait_ge(sem["prod_ready"], e)
                    for kf in range(KF):
                        a = e * FF + kf * P
                        mm = nc.tensor.matmul(bb[1][:, kf * S:(kf + 1) * S], g_sb[:, 1, a:a + P], xT, start=True, stop=True)
                    mm.then_inc(sem["h3_psum"], 1)
                if e >= 2:
                    j = e - 2
                    pe.wait_ge(sem["h_ready"], E + j + 1)
                    pe.wait_ge(sem["b2_taken"], 2)
                    if j >= 2:
                        pe.wait_ge(sem["y_added"], E + j - 1)
                    for t in range(NT):
                        for kf in range(KF):
                            a = (j * KF + kf) * P
                            mm = nc.tensor.matmul(bb[2 + j % 2][:, halves(t)], hs[:, j % 2, kf, halves(t)],
                                                  g_sb[:, 2, a:a + P], start=(kf == 0), stop=(kf == KF - 1))
                    mm.then_inc(sem["y_psum"], 1)
                yield "gexpert"
            yield "norm"
            yield "norm2"

        def turn_act(act, count):
            act.wait_ge(sem["xT_psum"], count)
            nc.scalar.activation(xT, bb[1][:, 0:S], ACT.Copy).then_inc(sem["xT_ready"], 1)

        def extra_gates(count):
            for label in GATE_SLOTS[count][1:]:
                yield label

        def gate_act(act, count, shifts):
            for n, label in zip(shifts, GATE_SLOTS[count]):
                act.wait_ge(sem["shifted"], n)
                nc.scalar.activation(g8[:, 3, :], g8[:, 3, :], ACT.Exp).then_inc(sem["shifted_exp"], 1)
                yield label
            yield GATE_SLOTS[count][-1]
            act.wait_ge(sem["combT_psum"], count)
            nc.scalar.activation(combT[:, :], bb[3][0:E, 0:S], ACT.Copy).then_inc(sem["combT_ready"], 1)
            yield "combT"
            yield "b2"

        def back_act(act):
            yield "norm"
            yield "norm2"
            yield "start"
            yield from gate_act(act, 1, (1,))
            for e in range(E + 1):
                if e < E:
                    act.wait_ge(sem["h_psum"], e + 1)
                    if e >= 2:
                        act.wait_ge(sem["y_psum"], e - 1)
                    for kf in range(KF):
                        n = e * KF + kf
                        ins = nc.scalar.activation(hs[:, e % 2, kf, :], bb[e % 2][:, kf * S:(kf + 1) * S], ACT.Relu,
                                                   bias=c("f_b1")[:, n:n + 1])
                    ins.then_inc(sem["h_ready"], 1)
                yield "expert"
            yield "norm"
            yield "norm2"
            turn_act(act, 1)
            yield "turn"
            act.wait_ge(sem["xz_psum"], 1)
            nc.scalar.activation(convbuf[:, :, 1:S + 1], bb[0][:, :].rearrange("p (a t) -> p a t", a=2),
                                 ACT.Copy).then_inc(sem["xz_copied"], 1)
            yield "dproj"
            for a in range(2):
                act.wait_ge(sem["conv_done"], a + 1)
                nc.scalar.activation(d_s[:, a, :], d_c[:, a, :], ACT.Silu, bias=c("d_cb")[:, a:a + 1]).then_inc(sem["silu_done"], 1)
            yield "conv"
            act.wait_ge(sem["g_psum"], 1)
            nc.scalar.activation(d_gs.rearrange("p t h v -> p (t h v)"), bb[3][:, 0:NT * VD], ACT.Silu).then_inc(sem["gate_silu"], 1)
            for t in range(NT):
                act.wait_ge(sem["kqv_psum"], t + 1)
                nc.scalar.activation(d_sq[:, t * 2 * QK:(t + 1) * 2 * QK], bb[1 + t][:, 0:2 * QK], ACT.Square).then_inc(sem["squares_done"], 1)
            yield "dtok"
            yield "dtok2"
            act.wait_ge(sem["gates_in"], 1)
            nc.scalar.activation(d_sm[:, 3], d_sm[:, 3], ACT.Exp).then_inc(sem["gates_exp"], 1)
            yield "dgates"
            act.wait_ge(sem["gates_one"], 1)
            nc.scalar.activation(d_sm[:, 4, :, 0:HD], d_sm[:, 3, :, 0:HD], ACT.Ln).then_inc(sem["gates_ln"], 1)
            yield "dgates2"
            yield "dgates3"
            for t in range(NT):
                yield "gm"
                act.wait_ge(sem["decay_psum"], t + 1)
                nc.scalar.activation(d_E.rearrange("p h t -> p (h t)"), bb[0][:, :], ACT.Exp).then_inc(sem["decay_exp"], 1)
                act.wait_ge(sem["kqT_psum"], t + 1)
                nc.scalar.activation(d_kqT, bb[1][:, 0:3 * P].rearrange("p (a b) -> p a b", a=3), ACT.Copy).then_inc(sem["kqT_ready"], 1)
                if t:
                    act.wait_ge(sem["cum_psum"], 1)
                    nc.scalar.activation(d_sm[:, 6, 0, 0:HD], bb[2][:, 0:HD], ACT.Exp).then_inc(sem["cum_exp"], 1)
                yield "decay"
                yield "kk"
                for l in range(LEVELS):
                    if l:
                        for g in range(2):
                            act.wait_ge(sem["p_psum"], 2 * (LEVELS * t + l) + g + 1)
                            nc.scalar.activation(d_P[:, 2 * g:2 * g + 2, :].rearrange("p h t -> p (h t)"), bb[3 * g][:, 0:2 * P],
                                                 ACT.Copy).then_inc(sem["p_copied"], 1)
                    yield "level"
                    yield "level2"
                yield "u"
                act.wait_ge(sem["o_ready"], t + 1)
                nc.scalar.activation(d_sq[:, 0:VD], d_o.rearrange("p h v -> p (h v)"), ACT.Square).then_inc(sem["o_squared"], 1)
                yield "o"
                yield "o2"
                yield "o3"
                act.wait_ge(sem["oTd_psum"], t + 1)
                nc.scalar.activation(d_oT[:, 0, :], bb[2][:, 0:P], ACT.Copy)
                nc.scalar.activation(d_oT[0:VD - P, 1, :], bb[2][0:VD - P, P:2 * P], ACT.Copy).then_inc(sem["oTd_ready"], 1)
                yield "oT"
                yield "dout"
            yield "norm"
            yield "norm2"
            turn_act(act, 2)
            yield "turn"
            for a in range(2):
                act.wait_ge(sem["clipped"], a + 1)
                nc.scalar.activation(p_t[:, a, :], p_t[:, a, :], ACT.Exp).then_inc(sem["clipped_exp"], 1)
            yield "prefix"
            yield "prefix2"
            yield "prefix3"
            yield "pout"
            yield "norm2"
            turn_act(act, 3)
            yield "turn"
            yield from gate_act(act, 2, (2, 3))
            for e in range(E + NSH + 2):
                if e < E + NSH:
                    act.wait_ge(sem["h_psum"], E + e + 1)
                    if e >= 2:
                        act.wait_ge(sem["h_ready"], E + e - 1)
                    b1 = c("g_b1") if e < E else c("g_bs1")
                    for kf in range(KF):
                        n = (e if e < E else e - E) * KF + kf
                        ins = nc.scalar.activation(h1s[:, e % 2, kf, :], bb[0][:, kf * S:(kf + 1) * S], ACT.Identity,
                                                   bias=b1[:, n:n + 1])
                    ins.then_inc(sem["h1_ready"], 1)
                if 1 <= e <= E + NSH:
                    j = e - 1
                    act.wait_ge(sem["prod_ready"], j + 1)
                    if j >= 2:
                        act.wait_ge(sem["y_psum"], E + j - 1)
                    nc.scalar.activation(hs[:, j % 2], h1s[:, j % 2], ACT.Silu).then_inc(sem["h_ready"], 1)
                yield "gexpert"
            yield "norm"
            yield "norm2"

        def top2_dve(dve, chain, src, shift):
            for t in range(NT):
                ins = nc.vector.max(mx8[:, t, :], src[:, t * E:(t + 1) * E])
            chain(ins)
            chain(nc.vector.tensor_copy(rep8[:, :, 0:2], mx8[:, :, 0:2]))
            for t in range(NT):
                one = slice(t * E, (t + 1) * E)
                nc.vector.match_replace(g8[:, 1, one], rep8[:, t, :], src[:, one], -BIG)
                ins = nc.vector.tensor_scalar(g8[:, 3, one], src[:, one], mx8[:, t, 0:1], None, ALU.subtract)
            ins.then_inc(sem["shifted"], 1)
            dve.wait_ge(sem["shifted"], shift)
            chain(nc.vector.tensor_tensor(g8[:, 2, :], g8[:, 1, :], src, ALU.not_equal))

        def top2_rest_dve(dve, chain, shift):
            dve.wait_ge(sem["shifted_exp"], shift)
            chain(nc.vector.tensor_tensor(g8[:, 4, :], g8[:, 3, :], g8[:, 2, :], ALU.mult))
            share_dve(chain, g8[:, 4, :], g8[:, 4, :]).then_inc(sem["comb_ready"], 1)

        def share_dve(chain, dst, src):
            s8 = src.rearrange("p (t e) -> p t e", t=NT)
            tot = g8[:, 6, 0:NT]
            chain(nc.vector.tensor_reduce(tot, s8, AX.X, ALU.add))
            chain(nc.vector.reciprocal(tot, tot))
            return nc.vector.tensor_tensor(dst.rearrange("p (t e) -> p t e", t=NT), s8,
                                           tot.unsqueeze(2).to_broadcast([P, NT, E]), ALU.mult)

        def back_norm_dve(dve, chain, count, label="norm"):
            src = handoff if count == 1 else xb
            stats_dve(chain, src, b_stat, b_mv, "back_var")
            yield label
            if count == 1:
                dve.wait_ge(lasting["stored"], 16)
            norm_dve(dve, xb, src, b_mv, "back_rstd", count).then_inc(sem["normed"], 1)
            yield "norm2"

        def back_dve(dve, chain):
            xf = xb[:, :, :].rearrange("p t d -> p (t d)")
            yield from back_norm_dve(dve, chain, 1)
            dve.wait_ge(sem["cxT_psum"], 1)
            dve.wait_ge(sem["cT_psum"], 1)
            nc.vector.tensor_copy(cxT[:, :, :].rearrange("p a s -> p (a s)"), bb[0][:, :]).then_inc(sem["cxT_ready"], 1)
            yield "start"
            dve.wait_ge(sem["logits_psum"], 1)
            chain(nc.vector.tensor_tensor(g8[:, 0, :].rearrange("p (t e) -> p t e", t=NT),
                                          bb[2][:, 0:NT * E].rearrange("p (t e) -> p t e", t=NT),
                                          c("f_bg").unsqueeze(1).to_broadcast([P, NT, E]), ALU.add))
            top2_dve(dve, chain, g8[:, 0, :], 1)
            yield "gate"
            top2_rest_dve(dve, chain, 1)
            yield "gate2"
            yield "combT"
            dve.wait_ge(sem["b2_psum"], 1)
            nc.vector.tensor_tensor(xf, bb[2][:, 0:S], xf, ALU.add).then_inc(sem["b2_taken"], 1)
            dve.wait_ge(sem["b2_taken"], 1)
            yield "b2"
            for e in range(E + 1):
                if e:
                    add_expert(dve, e - 1, e - 1)
                yield "expert"
            dve.wait_ge(sem["y_added"], E)
            yield from back_norm_dve(dve, chain, 2)
            yield "turn"
            yield "dproj"
            dve.wait_ge(sem["xz_copied"], 1)
            dve.wait_ge(sem["conv_zeroed"], 1)
            for a in range(2):
                w = c("d_cw")[:, a * CONV:(a + 1) * CONV]
                chain(nc.vector.tensor_scalar(d_c[:, a, :], convbuf[:, a, 0:S], w[:, 0:1], None, ALU.mult))
                for j in range(1, CONV):
                    ins = nc.vector.scalar_tensor_tensor(d_c[:, a, :], convbuf[:, a, j:j + S], w[:, j:j + 1], d_c[:, a, :],
                                                         ALU.mult, ALU.add)
                    if j < CONV - 1:
                        chain(ins)
                ins.then_inc(sem["conv_done"], 1)
            yield "conv"
            yield "dtok"
            for t in range(NT):
                dve.wait_ge(sem["squares_done"], t + 1)
                chain(nc.vector.tensor_reduce(d_sm[:, 0, t, :], d_sq[:, t * 2 * QK:(t + 1) * 2 * QK].rearrange("p (h d) -> p h d", d=DK), AX.X, ALU.add))
                nc.vector.tensor_scalar(d_sm[:, 0, t, :], d_sm[:, 0, t, :], L2_EPS, None, ALU.add).then_inc(sem["sums_in"], 1)
                ins = nc.vector.tensor_tensor(d_sm[:, 1, t, :], bb[1 + t][:, 2 * QK + VD:2 * QK + VD + 2 * HD],
                                              c("d_bias"), ALU.add)
            chain(ins)
            yield "dtok2"
            chain(nc.vector.tensor_scalar(d_sm[:, 2], d_sm[:, 1], -1.0, None, ALU.mult))
            nc.vector.tensor_copy(d_sm[:, 3, :, HD:], d_sm[:, 2, :, HD:])
            nc.vector.tensor_tensor(d_sm[:, 3, :, 0:HD], d_sm[:, 1, :, 0:HD], d_sm[:, 2, :, 0:HD], ALU.min).then_inc(sem["gates_in"], 1)
            yield "dgates"
            dve.wait_ge(sem["gates_exp"], 1)
            nc.vector.tensor_scalar(d_sm[:, 3], d_sm[:, 3], 1.0, None, ALU.add).then_inc(sem["gates_one"], 1)
            dve.wait_ge(sem["gates_one"], 1)
            nc.vector.reciprocal(d_sm[:, 4, :, HD:], d_sm[:, 3, :, HD:])
            yield "dgates2"
            dve.wait_ge(sem["gates_ln"], 1)
            chain(nc.vector.scalar_tensor_tensor(d_sm[:, 5, :, 0:HD], d_sm[:, 1, :, 0:HD], 0.0, d_sm[:, 4, :, 0:HD],
                                                 ALU.max, ALU.add))
            nc.vector.tensor_tensor(d_sm[:, 5, :, 0:HD], d_sm[:, 5, :, 0:HD],
                                    neg_a[:, :].unsqueeze(1).to_broadcast([P, NT, HD]), ALU.mult).then_inc(sem["gates_ready"], 1)
            for t in range(NT):
                dve.wait_ge(sem["sums_out"], t + 1)
                beta = d_sm[:, 4, t, HD:]
                for part, first in ((0, QK), (1, 0)):
                    ins = nc.vector.tensor_tensor(kqb[:, t, part, :, 0:DK],
                                                  bb[1 + t][:, first:first + QK].rearrange("p (h d) -> p h d", d=DK),
                                                  d_sm[:, 0, t, first // DK:first // DK + HD].unsqueeze(2).to_broadcast([P, HD, DK]),
                                                  ALU.mult)
                chain(ins)
                nc.vector.tensor_tensor(d_r[:, t], bb[1 + t][:, 2 * QK:2 * QK + VD].rearrange("p (h v) -> p h v", v=DV),
                                        beta.unsqueeze(2).to_broadcast([P, HD, DV]), ALU.mult)
                ins = nc.vector.tensor_tensor(kqb[:, t, 2], kqb[:, t, 0], beta.unsqueeze(2).to_broadcast([P, HD, DKP]), ALU.mult)
                ins.then_inc(sem["kqb_ready"], 1)
            yield "dgates3"
            for t in range(NT):
                dve.wait_ge(sem["gates_ready"], 1)
                up = c("upper").unsqueeze(1).to_broadcast([P, HD, P])
                if t:
                    dve.wait_ge(sem["p_psum"], 2 * LEVELS * t)
                nc.vector.tensor_tensor(d_Bm, up, d_sm[:, 5, t, 0:HD].unsqueeze(2).to_broadcast([P, HD, P]),
                                        ALU.mult).then_inc(sem["gm_ready"], 1)
                yield "gm"
                yield "decay"
                dve.wait_ge(sem["decay_exp"], t + 1)
                nc.vector.tensor_tensor(d_E, d_E, up, ALU.mult).then_inc(sem["decay_ready"], 1)
                dve.wait_ge(sem["decay_ready"], t + 1)
                for h in range(HD):
                    dve.wait_ge(sem["kk_psum"], HD * t + h + 1)
                    nc.vector.tensor_tensor(d_MA[:, h], bb[h][:, 0:2 * P].rearrange("p (a t) -> p a t", a=2),
                                            d_E[:, h, :].unsqueeze(1).to_broadcast([P, 2, P]), ALU.mult).then_inc(sem["ma_ready"], 1)
                yield "kk"
                if t:
                    dve.wait_ge(sem["ks_psum"], 1)
                    dve.wait_ge(sem["cum_exp"], 1)
                    for a in range(2):
                        ins = nc.vector.tensor_tensor(d_t[:, a], bb[3][:, a * VD:(a + 1) * VD].rearrange("p (h v) -> p h v", v=DV),
                                                      d_sm[:, 6, 0, 0:HD].unsqueeze(2).to_broadcast([P, HD, DV]), ALU.mult)
                    chain(ins)
                    nc.vector.tensor_tensor(d_r[:, t], d_r[:, t], d_t[:, 0], ALU.subtract).then_inc(sem["r_ready"], 1)
                else:
                    dve.wait_ge(sem["kqb_ready"], 1)
                eye = ident.unsqueeze(1).to_broadcast([P, HD // 2, P])
                for l in range(LEVELS):
                    if l == 0:
                        dve.wait_ge(sem["bm_ready"], LEVELS * t + 1)
                        for g in range(2):
                            nc.vector.tensor_tensor(d_X[:, g, 1], eye, d_Bm[:, 2 * g:2 * g + 2, :], ALU.subtract)
                            dve.wait_ge(sem["p_psum"], 2 * LEVELS * t + g + 1)
                            nc.vector.tensor_tensor(d_X[:, g, 0], eye, bb[3 * g][:, 0:2 * P].rearrange("p (h t) -> p h t", t=P),
                                                    ALU.subtract).then_inc(sem["x_updated"], 1)
                    yield "level"
                    if l:
                        for g in range(2):
                            dve.wait_ge(sem["y2_psum"], 2 * ((LEVELS - 1) * t + l - 1) + g + 1)
                            dve.wait_ge(sem["x_updated"], 2 * (LEVELS * t + l - 1) + g + 1)
                            first = 0 if l < LEVELS - 1 else 1
                            xg = d_X[:, g, first:2].rearrange("p a h t -> p (a h t)")
                            nc.vector.tensor_tensor(xg, xg, bb[1 + g][:, first * 2 * P:4 * P], ALU.subtract).then_inc(sem["x_updated"], 1)
                    yield "level2"
                dve.wait_ge(sem["u_psum"], t + 1)
                nc.vector.tensor_copy(d_u.rearrange("p h v -> p (h v)"), bb[0][:, 0:VD]).then_inc(sem["u_ready"], 1)
                yield "u"
                dve.wait_ge(sem["o_psum"], t + 1)
                of = d_o.rearrange("p h v -> p (h v)")
                if t:
                    nc.vector.tensor_tensor(of, bb[1][:, 0:VD], d_t[:, 1].rearrange("p h v -> p (h v)"), ALU.add).then_inc(sem["o_ready"], 1)
                else:
                    nc.vector.tensor_copy(of, bb[1][:, 0:VD]).then_inc(sem["o_ready"], 1)
                    dve.wait_ge(sem["st_psum"], 1)
                    nc.vector.tensor_tensor(d_st, bb[3][:, 0:VD], c("blockmask"), ALU.mult).then_inc(sem["st_ready"], 1)
                yield "o"
                dve.wait_ge(sem["o_squared"], t + 1)
                chain(nc.vector.tensor_reduce(d_sm[:, 7, t, 0:HD], d_sq[:, 0:VD].rearrange("p (h v) -> p h v", v=DV), AX.X, ALU.add))
                nc.vector.tensor_scalar(d_sm[:, 7, t, 0:HD], d_sm[:, 7, t, 0:HD], 1.0 / DV, LN_EPS, ALU.mult,
                                        ALU.add).then_inc(sem["sums_in"], 1)
                yield "o2"
                dve.wait_ge(sem["sums_out"], NT + t + 1)
                chain(nc.vector.tensor_tensor(d_o, d_o, d_sm[:, 7, t, 0:HD].unsqueeze(2).to_broadcast([P, HD, DV]), ALU.mult))
                dve.wait_ge(sem["gate_scaled"], 1)
                nc.vector.tensor_tensor(d_o, d_o, d_gs[:, t], ALU.mult).then_inc(sem["o_gated"], 1)
                yield "o3"
                yield "oT"
                dve.wait_ge(sem["layer_psum"], 1 + t)
                nc.vector.tensor_tensor(xb[:, t, :], bb[3][:, 0:P], xb[:, t, :], ALU.add).then_inc(sem["tile_added"], 1)
                yield "dout"
            dve.wait_ge(sem["tile_added"], NT)
            yield from back_norm_dve(dve, chain, 3)
            yield "turn"
            dve.wait_ge(sem["pkv_psum"], 1)
            nc.vector.tensor_scalar(p_t[:, 0, :], bb[0][:, 0:S], 0.0, None, ALU.min).then_inc(sem["clipped"], 1)
            dve.wait_ge(sem["pq_psum"], 1)
            nc.vector.tensor_scalar(p_t[:, 1, :], bb[2][:, 0:S], 0.0, None, ALU.min).then_inc(sem["clipped"], 1)
            yield "prefix"
            for a in range(2):
                dve.wait_ge(sem["clipped_exp"], a + 1)
                ins = nc.vector.scalar_tensor_tensor(p_k[:, a, :], bb[2 * a][:, 0:S], 0.0, p_t[:, a, :], ALU.max, ALU.add)
            chain(ins)
            chain(nc.vector.tensor_tensor(p_kv, bb[0][:, S:2 * S], p_k[:, 0, :], ALU.mult))
            one = c("ones")[:, 0:1].to_broadcast([P, S])
            nc.vector.tensor_tensor_scan(p_kp, one, p_k[:, 0, :], 0.0, ALU.mult, ALU.add)
            chain(nc.vector.tensor_tensor_scan(p_vp, one, p_kv, 0.0, ALU.mult, ALU.add))
            yield "prefix2"
            nc.vector.reciprocal(p_kp, p_kp)
            chain(nc.vector.tensor_tensor(p_vp, p_vp, p_kv, ALU.add))
            chain(nc.vector.tensor_tensor(p_vp, p_vp, p_kp, ALU.mult))
            nc.vector.tensor_tensor(p_vp, p_vp, p_k[:, 1, :], ALU.mult).then_inc(sem["prefix_done"], 1)
            yield "prefix3"
            dve.wait_ge(sem["layer_psum"], 1 + NT)
            chain(nc.vector.tensor_tensor(xf, bb[3][:, 0:S], xf, ALU.add))
            yield from back_norm_dve(dve, chain, 4, "pout")
            yield "turn"
            dve.wait_ge(sem["logits_psum"], 2)
            chain(nc.vector.tensor_copy(g8[:, 0, :], bb[2][:, 0:NT * E]))
            for t in range(NT):
                ins = nc.vector.max(mx8[:, t, :], g8[:, 0, t * E:(t + 1) * E])
            chain(ins)
            for t in range(NT):
                ins = nc.vector.tensor_scalar(g8[:, 3, t * E:(t + 1) * E], g8[:, 0, t * E:(t + 1) * E], mx8[:, t, 0:1],
                                              None, ALU.subtract)
            ins.then_inc(sem["shifted"], 1)
            yield "gate"
            dve.wait_ge(sem["shifted_exp"], 2)
            chain(share_dve(chain, g8[:, 5, :], g8[:, 3, :]))
            top2_dve(dve, chain, g8[:, 5, :], 3)
            yield "gate2"
            top2_rest_dve(dve, chain, 3)
            yield "gate3"
            yield "combT"
            dve.wait_ge(sem["b2_psum"], 2)
            dve.wait_ge(sem["xT_psum"], 3)
            chain(nc.vector.tensor_tensor(xf, bb[2][:, 0:S], xf, ALU.add))
            nc.vector.tensor_tensor(xb[:, :, :], xb[:, :, :], c("g_bs2").unsqueeze(1).to_broadcast([P, NT, D]),
                                    ALU.add).then_inc(sem["b2_taken"], 1)
            dve.wait_ge(sem["b2_taken"], 2)
            yield "b2"
            for e in range(E + NSH + 2):
                if e < E + NSH:
                    dve.wait_ge(sem["h1_ready"], e + 1)
                    dve.wait_ge(sem["h3_psum"], e + 1)
                    b3 = c("g_b3") if e < E else c("g_bs3")
                    for kf in range(KF):
                        n = (e if e < E else e - E) * KF + kf
                        ins = nc.vector.scalar_tensor_tensor(h1s[:, e % 2, kf, :], bb[1][:, kf * S:(kf + 1) * S],
                                                             b3[:, n:n + 1], h1s[:, e % 2, kf, :], ALU.add, ALU.mult)
                    ins.then_inc(sem["prod_ready"], 1)
                if e >= 2:
                    add_expert(dve, e - 2, E + e - 2)
                yield "gexpert"
            dve.wait_ge(sem["y_added"], 2 * E + NSH)
            yield from back_norm_dve(dve, chain, 5)

        def add_expert(dve, e, count):
            dve.wait_ge(sem["y_psum"], count + 1)
            if count:
                dve.wait_ge(sem["y_added"], count)
            bank = bb[2 + e % 2]
            if e < E:
                for t in range(NT):
                    ins = nc.vector.scalar_tensor_tensor(xb[:, t, :], bank[:, halves(t)], g8[:, 4, t * E + e:t * E + e + 1],
                                                         xb[:, t, :], ALU.mult, ALU.add)
            else:
                xf = xb[:, :, :].rearrange("p t d -> p (t d)")
                ins = nc.vector.tensor_tensor(xf, bank[:, 0:S], xf, ALU.add)
            ins.then_inc(sem["y_added"], 1)

        def back_pool(gps):
            norm_pool(gps, b_mv, "back_var", "back_rstd", 1)
            yield "norm"
            yield "norm2"
            yield "start"
            yield "gate"
            yield from extra_gates(1)
            yield "combT"
            yield "b2"
            for e in range(E + 1):
                yield "expert"
            norm_pool(gps, b_mv, "back_var", "back_rstd", 2)
            yield "norm"
            yield "norm2"
            yield "turn"
            gps.wait_ge(sem["normed"], 2)
            nc.gpsimd.memset(convbuf[:, :, 0:1], 0.0)
            nc.gpsimd.memset(convbuf[:, :, S + 1:S + CONV - 1], 0.0).then_inc(sem["conv_zeroed"], 1)
            yield "dproj"
            yield "conv"
            yield "dtok"
            for t in range(NT):
                gps.wait_ge(sem["sums_in"], t + 1)
                nc.gpsimd.tensor_tensor(d_sm[:, 0, t, :], d_sm[:, 0, t, :], mhalf[:, :], ALU.pow).then_inc(sem["sums_out"], 1)
            yield "dtok2"
            gps.wait_ge(sem["gate_silu"], 1)
            nc.gpsimd.tensor_tensor(d_gs.rearrange("p t h v -> p (t h) v"), d_gs.rearrange("p t h v -> p (t h) v"),
                                    c("d_gn").unsqueeze(1).to_broadcast([P, NT * HD, DV]), ALU.mult).then_inc(sem["gate_scaled"], 1)
            yield "dgates"
            yield "dgates2"
            yield "dgates3"
            for t in range(NT):
                yield "gm"
                yield "decay"
                if t == 0:
                    gps.wait_ge(sem["decay_ready"], 1)
                    gps.wait_ge(sem["kqb_ready"], 1)
                    nc.gpsimd.tensor_tensor(d_kh, kqb[:, t, 0], d_E[:, :, P - 1].unsqueeze(2).to_broadcast([P, HD, DKP]),
                                            ALU.mult).then_inc(sem["kh_ready"], 1)
                yield "kk"
                for l in range(LEVELS):
                    if l == 0:
                        gps.wait_ge(sem["ma_ready"], HD * (t + 1))
                        gps.wait_ge(sem["decay_psum"], t + 1)
                    else:
                        gps.wait_ge(sem["p_psum"], 2 * (LEVELS * t + l))
                        if l == 1:
                            gps.wait_ge(sem["x_updated"], 2 * (LEVELS * t + 1))
                    nc.gpsimd.tensor_tensor(d_Bm, d_MA[:, :, 1, :], c("levels")[:, halves(l)].unsqueeze(1).to_broadcast([P, HD, P]),
                                            ALU.mult).then_inc(sem["bm_ready"], 1)
                    yield "level"
                    yield "level2"
                yield "u"
                yield "o"
                gps.wait_ge(sem["sums_in"], NT + t + 1)
                nc.gpsimd.tensor_tensor(d_sm[:, 7, t, 0:HD], d_sm[:, 7, t, 0:HD], mhalf[:, 0:HD], ALU.pow).then_inc(sem["sums_out"], 1)
                yield "o2"
                yield "o3"
                yield "oT"
                yield "dout"
            norm_pool(gps, b_mv, "back_var", "back_rstd", 3)
            yield "norm"
            yield "norm2"
            yield "turn"
            yield "prefix"
            yield "prefix2"
            yield "prefix3"
            norm_pool(gps, b_mv, "back_var", "back_rstd", 4)
            yield "pout"
            yield "norm2"
            yield "turn"
            yield "gate"
            yield from extra_gates(2)
            yield "combT"
            yield "b2"
            for e in range(E + NSH + 2):
                yield "gexpert"
            norm_pool(gps, b_mv, "back_var", "back_rstd", 5)
            yield "norm"
            yield "norm2"

        def alternate(front, back):
            threads = {"front": front, "back": back}
            done = {"front": 0, "back": 0}
            for n, turn in enumerate(TURNS):
                name = ("front", "back")[n % 2]
                for _ in range(turn if threads[name] is not None else 0):
                    label = next(threads[name])
                    assert label == SLOTS[name][done[name]], (label, done, SLOTS[name][done[name]])
                    done[name] += 1
            for name, g in threads.items():
                assert g is None or next(g, None) is None and done[name] == len(SLOTS[name])

        SLOTS = {"front": [k for u in uses for k in [*earlier_slots(u), u[0]] if ends_slot(u)] + ["norm", "norm2", "xstart", "xproj"] + ["head"] * (HX + 3) + ["xout"]}
        tile_slots = ["gm", "decay", "kk"] + ["level", "level2"] * LEVELS + ["u", "o", "o2", "o3", "oT", "dout"]
        SLOTS["back"] = (["norm", "norm2", "start"] + GATE_SLOTS[1] + ["combT", "b2"] + ["expert"] * (E + 1)
                         + ["norm", "norm2", "turn", "dproj", "conv", "dtok", "dtok2", "dgates", "dgates2", "dgates3"]
                         + tile_slots * NT + ["norm", "norm2", "turn", "prefix", "prefix2", "prefix3", "pout", "norm2", "turn"]
                         + GATE_SLOTS[2] + ["combT", "b2"] + ["gexpert"] * (E + NSH + 2) + ["norm", "norm2"])

        def clear():
            with nc.Block() as block:
                @block.gpsimd
                def _(gps):
                    gps.sem_clear(range(numbers[0], numbers[-1] + 1))

        def chained(eng, name):
            count = [0]

            def chain(ins):
                count[0] += 1
                ins.then_inc(sem[name], 1)
                eng.wait_ge(sem[name], count[0])
            return chain

        def tokens(a):
            return a.rearrange("(t p) d -> p t d", p=P)

        def batches(front, back, after):
            with nc.Block() as block:
                @block.sync
                def _(sp):
                    if front is not None:
                        if back is not None:
                            sp.wait_ge(sem["cT_psum"], 1)
                        sp.dma_start(ctx_in[:, :, :], tokens(ctx[front])).then_inc(sem["ctx_loaded"], 16)
                    if after is not None:
                        sp.wait_ge(sem["front_done"], 1)
                        sp.dma_start(x_in[:, :, :], tokens(x[after])).then_inc(sem["x_loaded"], 16)
                        sp.wait_ge(sem["x1T_psum"], 1)
                        sp.dma_start(a_ctx[:, :, :], tokens(ctx[after])).then_inc(sem["a_ctx_loaded"], 16)
                        sp.wait_ge(sem["x_loaded"], 16)
                        sp.wait_ge(sem["a_ctx_loaded"], 16)
                    if front is not None:
                        sp.wait_ge(sem["ctx_loaded"], 16)
                    if back is not None:
                        sp.wait_ge(sem["normed"], 5)
                        sp.sem_clear(lasting["stored"])
                        sp.dma_start(tokens(out[back]), xb[:, :, :]).then_inc(lasting["stored"], 16)
                    if front is None:
                        sp.wait_ge(lasting["stored"], 16)
                    if back is None:
                        sp.wait_ge(lasting["experts_loaded"], 32)

                @block.tensor
                def _(pe):
                    alternate(front_pe(pe, back is None) if front is not None else None,
                              back_pe(pe) if back is not None else None)

                @block.scalar
                def _(act):
                    alternate(front_act(act) if front is not None else None, back_act(act) if back is not None else None)

                @block.vector
                def _(dve):
                    chain = chained(dve, "dve_chain")
                    alternate(front_dve(dve, chain, back is not None) if front is not None else None,
                              back_dve(dve, chain) if back is not None else None)

                @block.gpsimd
                def _(gps):
                    alternate(front_pool(gps) if front is not None else None, back_pool(gps) if back is not None else None)
            clear()

        with nc.Block() as block:
            @block.sync
            def _(sp):
                w3 = w_qkv.rearrange("p (w n) -> p w n", w=3)
                sp.dma_start(small_sb[:, :], small).then_inc(sem["weights_loaded"], 16)
                sp.dma_start(x_in[:, :, :], tokens(x[0])).then_inc(sem["x_loaded"], 16)
                sp.dma_start(a_ctx[:, :, :], tokens(ctx[0])).then_inc(sem["x_loaded"], 16)
                sp.dma_start(wqkv_sb[:, 1, :], w3[:, 1, :]).then_inc(sem["x_loaded"], 16)
                sp.dma_start(wqkv_sb[:, 0, :], w3[:, 0, :]).then_inc(lasting["qv_loaded"], 16)
                sp.dma_start(wqkv_sb[:, 2, :], w3[:, 2, :]).then_inc(lasting["qv_loaded"], 16)
                sp.dma_start(wo_sb[:, :, :], w_o.rearrange("p (j n) -> p j n", n=P)).then_inc(lasting["wo_loaded"], 16)
                sp.dma_start(f_sb[:, :, :], f_w.rearrange("p (w n) -> p w n", w=2)).then_inc(lasting["experts_loaded"], 16)
                sp.dma_start(g_sb[:, :, :], g_w.rearrange("p (w n) -> p w n", w=3)).then_inc(lasting["experts_loaded"], 16)
                sp.wait_ge(sem["x_loaded"], 48)

            @block.tensor
            def _(pe):
                pe.wait_ge(sem["weights_loaded"], 16)
                nc.tensor.matmul(bb[0][:, 0:P], c("d_wsoT")[:, 0:P], c("d_wtop"), start=True, stop=True)
                nc.tensor.matmul(bb[0][0:VD - P, P:2 * P], c("d_wsoT")[:, P:VD], c("d_wtop"), start=True,
                                 stop=True).then_inc(sem["wd_psum"], 1)

            @block.scalar
            def _(act):
                act.wait_ge(sem["weights_loaded"], 16)
                nc.scalar.activation(neg_a[:, :], c("d_alog"), ACT.Exp).then_inc(sem["alog_exp"], 1)

            @block.vector
            def _(dve):
                nc.vector.memset(mhalf[:, :], -0.5)
                nc.vector.memset(rep8[:, :, :], BIG).then_inc(lasting["stored"], 16)
                nc.vector.memset(kqb[:, :, :, :, :].rearrange("p a b c d -> p (a b c d)"), 0.0)
                dve.wait_ge(sem["alog_exp"], 1)
                nc.vector.tensor_scalar(neg_a[:, :], neg_a[:, :], -1.0, None, ALU.mult)
                dve.wait_ge(sem["wd_psum"], 1)
                nc.vector.tensor_copy(wd_sb[:, 0, :], bb[0][:, 0:P])
                nc.vector.tensor_copy(wd_sb[0:VD - P, 1, :], bb[0][0:VD - P, P:2 * P])
        clear()

        batches(0, None, 1)
        with nc.Fori(1, B - 1) as i:
            batches(i, i - 1, i + 1)
        batches(B - 1, B - 2, None)
        batches(None, B - 1, None)


def layouts(a):
    import numpy as np

    def rows(v):
        return np.broadcast_to(np.asarray(v).reshape(1, -1), (P, np.asarray(v).size))

    def cols(v):
        return np.asarray(v).reshape(-1, P).T

    def top(v):
        v = np.asarray(v)
        return np.concatenate([v, np.zeros((P - v.shape[0], v.shape[1]), v.dtype)], 0)

    p = np.arange(P)
    upper = (p[:, None] <= p[None, :]).astype(np.float32)
    strict = (p[:, None] > p[None, :]).astype(np.float32)
    levels = []
    for l in range(LEVELS):
        same = (p[:, None] >> (l + 1)) == (p[None, :] >> (l + 1))
        levels.append((same & ((p[:, None] >> l) % 2 == 0) & ((p[None, :] >> l) % 2 == 1)).astype(np.float32))
    block = np.zeros((P, HD, DV), np.float32)
    for h in range(HD):
        block[h * DKP:(h + 1) * DKP, h] = 1
    g = a.get
    conv = np.concatenate([g("L1_attn_conv_x_w")[:, 0, :], g("L1_attn_conv_z_w")[:, 0, :]], 1)
    parts = {
        "ident": np.eye(P, dtype=np.float32), "upper": upper, "strict": strict, "levels": np.concatenate(levels, 1),
        "headmask": (p[:, None] // DX == np.arange(HX)[None, :]).astype(np.float32),
        "fold": (p[:, None] % HALF == p[None, :] % HALF).astype(np.float32),
        "blockmask": block.reshape(P, VD), "ones": np.ones((P, P), np.float32), "bo": rows(g("L0_attn_bo")),
        "x_wq": g("L0_xattn_wq_w").T, "x_wk": g("L0_xattn_wk_w").T, "x_wv": g("L0_xattn_wv_w").T, "x_wo": g("L0_xattn_wo_w").T,
        "x_bq": cols(g("L0_xattn_wq_b")), "x_bk": cols(g("L0_xattn_wk_b")), "x_bv": rows(g("L0_xattn_wv_b")),
        "x_bo": rows(g("L0_xattn_wo_b")),
        "f_b1": cols(g("L0_ffn_b1")), "f_b2": top(g("L0_ffn_b2")), "f_wg": g("L0_ffn_Wg").T, "f_bg": rows(g("L0_ffn_bg")),
        "d_win": g("L1_attn_W_in"), "d_cw": conv,
        "d_cb": np.stack([g("L1_attn_conv_x_b"), g("L1_attn_conv_z_b")], 1),
        "d_wqkv": np.concatenate([g("L1_attn_W_q"), g("L1_attn_W_k"), g("L1_attn_W_v"), g("L1_attn_W_gk"), g("L1_attn_W_b")], 1),
        "d_wg": g("L1_attn_W_g"), "d_bias": rows(np.concatenate([g("L1_attn_dt_bias"), g("L1_attn_b_b")])),
        "d_alog": rows(g("L1_attn_A_log")), "d_gn": rows(g("L1_attn_g_norm_w")), "d_wsoT": g("L1_attn_W_so").T,
        "d_wtop": g("L1_attn_W_out")[0:P], "d_wbot": g("L1_attn_W_out")[P:2 * P],
        "p_wq": g("L1_xattn_Wq").T, "p_wk": g("L1_xattn_Wk").T, "p_wv": g("L1_xattn_Wv").T,
        "g_b1": cols(g("L1_ffn_b1")), "g_b3": cols(g("L1_ffn_b3")), "g_b2": top(g("L1_ffn_b2")), "g_wg": g("L1_ffn_Wg"),
        "g_bs1": cols(g("L1_ffn_bs1")), "g_bs3": cols(g("L1_ffn_bs3")), "g_bs2": rows(g("L1_ffn_bs2")),
    }
    assert all(parts[n].shape == (P, k) for n, k in SMALL), [(n, parts[n].shape, k) for n, k in SMALL if parts[n].shape != (P, k)]
    wo = g("L0_attn_Wo").reshape(HA, 2, HA // 2, D).transpose(1, 0, 2, 3).reshape(P, -1)

    def up(w, shared=None):
        w = w.transpose(1, 0, 2).reshape(D, -1)
        return w if shared is None else np.concatenate([w, shared], 1)

    def down(w, shared=None):
        w = w.reshape(-1, D)
        w = w if shared is None else np.concatenate([w, shared], 0)
        return w.reshape(-1, P, D).transpose(1, 0, 2).reshape(P, -1)

    return {
        "x": g("x"), "ctx": g("ctx_1024"),
        "small": np.concatenate([parts[n] for n, _ in SMALL], 1),
        "w_qkv": np.concatenate([g("L0_attn_Wq"), g("L0_attn_Wk"), g("L0_attn_Wv")], 1), "w_o": wo,
        "f_w": np.concatenate([up(g("L0_ffn_W1").transpose(0, 2, 1)), down(g("L0_ffn_W2").transpose(0, 2, 1))], 1),
        "g_w": np.concatenate([up(g("L1_ffn_W1"), g("L1_ffn_Ws1")), up(g("L1_ffn_W3"), g("L1_ffn_Ws3")),
                               down(g("L1_ffn_W2"), g("L1_ffn_Ws2"))], 1),
    }


def kernel(**inputs):
    import numpy as np
    import concourse.bacc as bacc
    from concourse.bass_utils import run_bass_kernel_spmd

    nc = bacc.Bacc("TRN2", target_bir_lowering=False, num_devices=1)
    arrays, args = {}, []
    for name, a in layouts({k: np.asarray(v) for k, v in inputs.items()}).items():
        a = np.ascontiguousarray(a)
        arrays[f"in_{name}"] = a
        args.append(nc.dram_tensor(f"in_{name}", a.shape, mybir.dt.from_np(a.dtype), kind="ExternalInput").ap())
    args.append(nc.dram_tensor("out", (B, S, D), F32, kind="ExternalOutput").ap())
    build(nc, *args)
    r = run_bass_kernel_spmd(nc, [arrays], core_ids=[0])
    return r.results[0]["out"]
```
